# Optimizing a Trainium2 kernel written in Bass

```python
import numpy as np
import jax
import jax.numpy as jnp

def _softmax(x, axis=-1):
    return jax.nn.softmax(x, axis=axis)

def _gelu(x):
    return jax.nn.gelu(x, approximate=True)

def _silu(x):
    return jax.nn.silu(x)

def _sigmoid(x):
    return jax.nn.sigmoid(x)

def _layernorm(x, axis=-1, eps=1e-05):
    m = jnp.mean(x, axis=axis, keepdims=True)
    v = jnp.var(x, axis=axis, keepdims=True)
    return (x - m) / jnp.sqrt(v + eps)

def _scatter_add(tgt, idx, src, axis=0):
    return tgt.at[idx].add(src)

def _segment_sum(src, seg, n):
    return jax.ops.segment_sum(src, seg, n)
kernel_name = 'mk_seq_preln_d1_jaxref_r4_62671c'

def setup_inputs(seed: int=0):
    np.random.seed(seed)
    _w = jnp.asarray

    def _L0_attn_setup():
        import jax, jax.numpy as jnp
        import numpy as np
        B_SZ, L, D_MODEL, D_STATE, DT_RANK = (4, 1024, 256, 16, 64)
        key = jax.random.key(seed)
        k_x, k_wx, k_wdt = jax.random.split(key, 3)
        x = jax.random.normal(k_x, (B_SZ, L, D_MODEL), dtype=jnp.float32)
        A_log = jnp.log(jnp.broadcast_to(jnp.arange(1, D_STATE + 1, dtype=jnp.float32), (D_MODEL, D_STATE)))
        D_param = jnp.ones((D_MODEL,), dtype=jnp.float32)
        W_x = jax.random.normal(k_wx, (DT_RANK + 2 * D_STATE, D_MODEL), dtype=jnp.float32) * 0.02
        W_dt = jax.random.normal(k_wdt, (D_MODEL, DT_RANK), dtype=jnp.float32) * 0.02
        b_dt = jnp.zeros((D_MODEL,), dtype=jnp.float32)
        return {'x': x, 'A_log': A_log, 'D_param': D_param, 'W_x': W_x, 'W_dt': W_dt, 'b_dt': b_dt}
    _L0_attn_in = _L0_attn_setup()

    def _L0_ffn_setup():
        import jax, jax.numpy as jnp
        import numpy as np
        HIDDEN = 256
        HEAD_DIM = 64
        N_EXPERTS = 16
        MIN_EXPERTS = 2
        B, T = (4, 512)

        def _normalize(x, axis):
            n = jnp.sqrt(jnp.sum(x * x, axis=axis, keepdims=True))
            return x / jnp.maximum(n, 1e-12)

        def _ste(x):
            hard = jax.lax.stop_gradient((x > 0).astype(x.dtype))
            return hard + x - jax.lax.stop_gradient(x)

        def _gating(hidden_states, sim_matrix, gates):
            b, t, c = hidden_states.shape
            flat = hidden_states.reshape(b * t, c)
            logits = _normalize(flat, -1) @ _normalize(sim_matrix, 0) - jax.nn.sigmoid(gates)
            gated = jax.nn.relu(logits)
            mask = _ste(gated)
            inactive = jnp.sum(mask, axis=1) == 0
            _, fb_idx = jax.lax.top_k(logits, MIN_EXPERTS)
            fb = jnp.zeros_like(mask).at[jnp.arange(b * t)[:, None], fb_idx].set(1.0)
            fb_applied = inactive[:, None] & (fb > 0)
            mask = jnp.where(fb_applied, 1.0, mask)
            masked_logits = jnp.where(mask > 0, gated, -jnp.inf)
            return jax.nn.softmax(masked_logits, axis=-1).reshape(b, t, -1)
        key = jax.random.key(seed)
        ks = jax.random.split(key, 6)
        xav_qkv = float(np.sqrt(6.0 / (HIDDEN + HEAD_DIM)))
        return {'hidden_states': jax.random.normal(ks[0], (B, T, HIDDEN), dtype=jnp.float32), 'sim_matrix': jax.random.normal(ks[1], (HIDDEN, N_EXPERTS), dtype=jnp.float32), 'gates': jnp.zeros((N_EXPERTS,), dtype=jnp.float32), 'q_proj': jax.random.uniform(ks[2], (N_EXPERTS, HIDDEN, HEAD_DIM), jnp.float32, -xav_qkv, xav_qkv), 'k_proj': jax.random.uniform(ks[3], (N_EXPERTS, HIDDEN, HEAD_DIM), jnp.float32, -xav_qkv, xav_qkv), 'v_proj': jax.random.uniform(ks[4], (N_EXPERTS, HIDDEN, HEAD_DIM), jnp.float32, -xav_qkv, xav_qkv), 'o_proj': jax.random.uniform(ks[5], (N_EXPERTS, HEAD_DIM, HIDDEN), jnp.float32, -xav_qkv, xav_qkv)}
    _L0_ffn_in = _L0_ffn_setup()
    _d = {'L0_attn_x': _L0_attn_in['x'], 'L0_attn_A_log': _L0_attn_in['A_log'], 'L0_attn_D_param': _L0_attn_in['D_param'], 'L0_attn_W_x': _L0_attn_in['W_x'], 'L0_attn_W_dt': _L0_attn_in['W_dt'], 'L0_attn_b_dt': _L0_attn_in['b_dt'], 'L0_ffn_sim_matrix': _L0_ffn_in['sim_matrix'], 'L0_ffn_gates': _L0_ffn_in['gates'], 'L0_ffn_q_proj': _L0_ffn_in['q_proj'], 'L0_ffn_k_proj': _L0_ffn_in['k_proj'], 'L0_ffn_v_proj': _L0_ffn_in['v_proj'], 'L0_ffn_o_proj': _L0_ffn_in['o_proj']}
    _x0 = _d['L0_attn_x']
    _d['L0_attn_x'] = jax.random.normal(jax.random.fold_in(jax.random.key(seed), 1), (16, 512, 256), dtype=_x0.dtype)
    del _x0
    return _d

def reference(L0_attn_x, L0_attn_A_log, L0_attn_D_param, L0_attn_W_x, L0_attn_W_dt, L0_attn_b_dt, L0_ffn_sim_matrix, L0_ffn_gates, L0_ffn_q_proj, L0_ffn_k_proj, L0_ffn_v_proj, L0_ffn_o_proj):

    def _L0_attn_ref(x, A_log, D_param, W_x, W_dt, b_dt):
        import jax, jax.numpy as jnp
        import numpy as np
        B_SZ, L, D_MODEL, D_STATE, DT_RANK = (4, 1024, 256, 16, 64)
        xp = jnp.einsum('bld,kd->blk', x, W_x)
        dt_lowrank = xp[..., :DT_RANK]
        B_params = xp[..., DT_RANK:DT_RANK + D_STATE]
        C_params = xp[..., DT_RANK + D_STATE:]
        dt = jax.nn.softplus(jnp.einsum('blr,dr->bld', dt_lowrank, W_dt) + b_dt)
        A = -jnp.exp(A_log)

        def step(h, inp):
            x_t, dt_t, B_t, C_t = inp
            A_bar = jnp.exp(dt_t[:, :, None] * A)
            h = A_bar * h + dt_t[:, :, None] * B_t[:, None, :] * x_t[:, :, None]
            y_t = jnp.einsum('bdn,bn->bd', h, C_t)
            return (h, y_t)
        h0 = jnp.zeros((x.shape[0], D_MODEL, D_STATE), dtype=x.dtype)
        xs = (x.swapaxes(0, 1), dt.swapaxes(0, 1), B_params.swapaxes(0, 1), C_params.swapaxes(0, 1))
        _, ys = jax.lax.scan(step, h0, xs)
        y = ys.swapaxes(0, 1)
        return y + x * D_param

    def _L0_ffn_ref(hidden_states, sim_matrix, gates, q_proj, k_proj, v_proj, o_proj):
        import jax, jax.numpy as jnp
        import numpy as np
        HIDDEN = 256
        HEAD_DIM = 64
        N_EXPERTS = 16
        MIN_EXPERTS = 2
        B, T = (4, 512)

        def _normalize(x, axis):
            n = jnp.sqrt(jnp.sum(x * x, axis=axis, keepdims=True))
            return x / jnp.maximum(n, 1e-12)

        def _ste(x):
            hard = jax.lax.stop_gradient((x > 0).astype(x.dtype))
            return hard + x - jax.lax.stop_gradient(x)

        def _gating(hidden_states, sim_matrix, gates):
            b, t, c = hidden_states.shape
            flat = hidden_states.reshape(b * t, c)
            logits = _normalize(flat, -1) @ _normalize(sim_matrix, 0) - jax.nn.sigmoid(gates)
            gated = jax.nn.relu(logits)
            mask = _ste(gated)
            inactive = jnp.sum(mask, axis=1) == 0
            _, fb_idx = jax.lax.top_k(logits, MIN_EXPERTS)
            fb = jnp.zeros_like(mask).at[jnp.arange(b * t)[:, None], fb_idx].set(1.0)
            fb_applied = inactive[:, None] & (fb > 0)
            mask = jnp.where(fb_applied, 1.0, mask)
            masked_logits = jnp.where(mask > 0, gated, -jnp.inf)
            return jax.nn.softmax(masked_logits, axis=-1).reshape(b, t, -1)
        b, t, c = hidden_states.shape
        rw = _gating(hidden_states, sim_matrix, gates)
        q = jnp.einsum('bte,bted->btd', rw, jnp.einsum('btc,ecd->bted', hidden_states, q_proj))
        k = jnp.einsum('bte,bted->btd', rw, jnp.einsum('btc,ecd->bted', hidden_states, k_proj))
        v = jnp.einsum('bte,bted->btd', rw, jnp.einsum('btc,ecd->bted', hidden_states, v_proj))
        scale = 1.0 / jnp.sqrt(jnp.asarray(HEAD_DIM, dtype=q.dtype))
        scores = jnp.einsum('bqd,bkd->bqk', q, k) * scale
        causal = jnp.tril(jnp.ones((t, t), dtype=bool))
        scores = jnp.where(causal, scores, -jnp.inf)
        attn = jnp.einsum('bqk,bkd->bqd', jax.nn.softmax(scores, axis=-1), v)
        mixed = attn[:, :, None, :] * rw[..., None]
        return jnp.einsum('bted,edc->btc', mixed, o_proj)
    x = L0_attn_x
    x = x + _L0_attn_ref(_layernorm(x, axis=-1), L0_attn_A_log, L0_attn_D_param, L0_attn_W_x, L0_attn_W_dt, L0_attn_b_dt)
    x = x + _L0_ffn_ref(_layernorm(x, axis=-1), L0_ffn_sim_matrix, L0_ffn_gates, L0_ffn_q_proj, L0_ffn_k_proj, L0_ffn_v_proj, L0_ffn_o_proj)
    return x

_drawn_inputs = setup_inputs


def setup_inputs(seed=0):
    import zlib

    import numpy as np

    out = dict(_drawn_inputs(seed))
    spreads = {'L0_attn_D_param': (1.0, 0.2), 'L0_attn_b_dt': (0.0, 0.717), 'L0_ffn_gates': (0.0, 0.276)}
    factors = {'L0_attn_W_dt': 8.0, 'L0_ffn_q_proj': 3.263, 'L0_ffn_k_proj': 3.229}
    for name, (base, spread) in spreads.items():
        noise = np.random.default_rng([zlib.crc32(name.encode()), seed]).standard_normal(out[name].shape)
        drawn = base * np.exp(spread * noise) if base else spread * noise
        out[name] = jnp.asarray(drawn.astype(out[name].dtype))
    for name, factor in factors.items():
        out[name] = (out[name] * factor).astype(out[name].dtype)
    return out
```

```python
from contextlib import ExitStack

import concourse.bass as bass
from concourse import mybir

ALU = mybir.AluOpType
ACT = mybir.ActivationFunctionType
F32 = mybir.dt.float32
F16 = mybir.dt.float16
BF16 = mybir.dt.bfloat16
AX_X = mybir.AxisListType.X

P = 128
NB, L, D = 16, 512, 256
NS, RANK = 16, 64
NE, HD = 16, 64
T = L // P
CH = D // P
QKV = 3 * HD
KO = NE * HD // P
EPS = 1e-5
NORM_MIN_SQ = 1e-24
SIM_SCALE = 64.0
W_TOP = 256.0
MASKED = -1e30

EXPERTS_AT = {5: [0], 6: [1, 2], 7: [3], 8: [4], 9: [5], 10: [6], 11: [7], 12: [8, 9], 13: [10, 11],
              14: [12, 13], 15: [14, 15]}

BANK_USES = (
    [("q", "attend"), ("s0", "attend"), ("s2", "attend"), ("xh", "project"), ("logit", "project"),
     ("pt1", "attend"), ("pv", "attend"), ("xn", "prepare"), ("dtl", "prepare"), ("dtp", "prepare"),
     ("dtT", "prepare"), ("mix0", "attend"), ("op0", "attend"), ("mix1", "attend"), ("op1", "attend"),
     ("mix2", "attend"), ("op2", "attend"), ("mix3", "attend"), ("op3", "attend")],
    [("k", "attend"), ("s1", "attend"), ("s3", "attend"), ("xh", "project"), ("pt0", "attend"),
     ("pt23", "attend"), ("xn", "prepare"), ("bc", "prepare"), ("dtp", "prepare"), ("dtT", "prepare"),
     ("mix0", "attend"), ("mix1", "attend"), ("mix2", "attend"), ("mix3", "attend")],
)


def stages_of(i):
    if not isinstance(i, int):
        return {"prepare", "scan", "project", "attend"}
    on = set()
    if -1 <= i <= NB - 2:
        on.add("prepare")
    if 0 <= i <= NB - 1:
        on.add("scan")
    if 1 <= i <= NB:
        on.add("project")
    if 2 <= i <= NB + 1:
        on.add("attend")
    return on


def bank_use(bank, i, what):
    if isinstance(i, int):
        before = {"prepare": min(i + 1, NB), "project": max(i - 1, 0), "attend": max(i - 2, 0)}
    else:
        before = {"prepare": i + 1, "project": i - 1, "attend": i - 2}
    uses = BANK_USES[bank]
    on = stages_of(i)
    inside = 0
    for name, stage in uses:
        if stage in on:
            inside += 1
        if name == what:
            break
    per = {s: sum(1 for _, stage in uses if stage == s) for s in before}
    if isinstance(i, int):
        return inside + sum(per[s] * before[s] for s in per)
    return i * len(uses) + (inside + per["prepare"] - per["project"] - 2 * per["attend"])


VEC_PREP = ["stats", "aggr", "var", "sq", "vsq", "cor", "rstd", "nmr"]
ACT_PREP = ["ln", "y0", "abs", "exp", "softplus"]
POOL_PREP = ["xn", "skip", "yinit"]
VEC_PROJ = ["stats", "aggr", "var", "sq", "vsq", "cor", "rstd", "nmr", "rr", "ss", "ssc", "y", "ysq", "yv",
            "ycor", "r"]
ACT_PROJ = ["ln", "y0", "ln2", "y2", "hi0", "hi1"]
VEC_GATE = ["top", "strict", "eq", "rank", "room", "fit", "take", "fb", "idle", "fbm", "mask", "gated", "gmax",
            "shift", "kept", "sum", "rsum", "rw", "rws"]
VEC_ATT = ["mx0", "nb0", "mx1", "nb1", "mx2", "nb2", "mx3", "nb3", "rinv", "rwn"]


def step(steps, name, b):
    return b * len(steps) + (steps.index(name) + 1)


def scan_attention_kernel(nc, x, A_log, D_param, WxT, WdtT, b_dt, sim, gates, Wqkv, Wo, out):
    with ExitStack() as ctx:
        def sb(name, shape, dt=F32):
            return ctx.enter_context(nc.sbuf_tensor(name, shape, dt))

        def bank(name):
            return ctx.enter_context(nc.psum_tensor(name, [P, 512], F32))

        def sem(name):
            return ctx.enter_context(nc.semaphore(name))

        ident = sb("ident", [P, P])
        identb = sb("identb", [P, P], BF16)
        causal = sb("causal", [P, P], BF16)
        ones = sb("ones", [P, P])
        restart = sb("restart", [P, T, NE])
        wx = sb("wx", [P, CH, RANK + 2 * NS])
        wdt = sb("wdt", [RANK + 1, D])
        negA = sb("negA", [P, CH, NS])
        dskip = sb("dskip", [P, D])
        sgate = sb("sgate", [P, NE])
        simf = sb("simf", [P, CH, NE])
        simsq = sb("simsq", [P, CH, NE])
        simhi = sb("simhi", [P, CH, NE], F16)
        simlo = sb("simlo", [P, CH, NE], F16)
        snorm = sb("snorm", [P, 4, NE])
        wmax = sb("wmax", [P, 4])
        wraw = sb("wraw", [P, CH, NE * QKV])
        whi = sb("whi", [P, CH, NE * QKV], F16)
        wlo = sb("wlo", [P, CH, NE * QKV], F16)
        wo = sb("wo", [P, KO, D])
        xt = sb("xt", [P, T, D])
        xn = sb("xn", [P, T, D])
        xnT = sb("xnT", [P, CH, L])
        dtl = sb("dtl", [RANK + 1, L])
        sp = sb("sp", [P, CH, L])
        dt_next = sb("dt_next", [P, CH, L])
        u_next = sb("u_next", [P, T, D])
        y_next = sb("y_next", [P, T, D])
        bc_next = sb("bc_next", [P, T, 2 * NS])
        st1 = sb("st1", [P, T, 6])
        mv1 = sb("mv1", [P, T, 2])
        sm1 = sb("sm1", [P, 6, T])
        dt = sb("dt", [P, CH, L])
        u = sb("u", [P, T, D])
        y = sb("y", [P, T, D])
        bcur = sb("bcur", [P, T, NS])
        ccur = sb("ccur", [P, T, NS])
        v = sb("v", [P, 2, T, D])
        abar = sb("abar", [P, 2, CH, L])
        h = sb("h", [P, 2, CH, L])
        x2a = sb("x2a", [P, T, D])
        xh = sb("xh", [P, T, D])
        xhi = sb("xhi", [P, CH, L], F16)
        xlo = sb("xlo", [P, CH, L], F16)
        st2 = sb("st2", [P, T, 6])
        mv2 = sb("mv2", [P, T, 2])
        sm2 = sb("sm2", [P, 14, T])
        lg = sb("lg", [P, T, NE])
        top8 = sb("top8", [P, T, 8])
        g1 = sb("g1", [P, 10, T, NE])
        gs = sb("gs", [P, 6, T])
        ex = sb("ex", [P, T, NE])
        rw = sb("rw", [P, T, NE])
        rws = sb("rws", [P, T, NE])
        acc = sb("acc", [P, T, QKV])
        qkv = sb("qkv", [P, T, QKV])
        x2b = sb("x2b", [P, T, D])
        qT = sb("qT", [HD, L])
        kT = sb("kT", [HD, L])
        mx = sb("mx", [P, T])
        nb = sb("nb", [P, T])
        rs = sb("rs", [P, T])
        rinv = sb("rinv", [P, T])
        rwn = sb("rwn", [P, T, NE])
        pr = sb("pr", [P, T, L])
        pt = sb("pt", [P, T, L])
        at = sb("at", [P, T, HD])
        mix = sb("mix", [P, 2, NE, HD])
        mixT = sb("mixT", [P, KO, P])
        outt = sb("outt", [P, T, D])

        dbu = [bank("dbu0"), bank("dbu1")]
        hT = [bank("hT0"), bank("hT1")]
        qb = [bank("qb0"), bank("qb1")]
        mb = [bank("mb0"), bank("mb1")]

        const_loaded = sem("const_loaded")
        pool_const = sem("pool_const")
        pool_wmax = sem("pool_wmax")
        vec_const = sem("vec_const")
        act_const = sem("act_const")
        pe_const = sem("pe_const")
        x_loaded = sem("x_loaded")
        dt_moved, u_moved, b_moved, c_moved = sem("dt_moved"), sem("u_moved"), sem("b_moved"), sem("c_moved")
        y_moved, x2a_moved, x2b_moved = sem("y_moved"), sem("x2a_moved"), sem("x2b_moved")
        out_stored = sem("out_stored")
        vec_prep, act_prep, pool_prep = sem("vec_prep"), sem("act_prep"), sem("pool_prep")
        v_done = sem("v_done")
        abar_done = sem("abar_done")
        dbu_full = sem("dbu_full")
        scan_done = sem("scan_done")
        hT_full = sem("hT_full")
        read_out = sem("read_out")
        vec_proj, act_proj, pool_proj = sem("vec_proj"), sem("act_proj"), sem("pool_proj")
        vec_gate, act_gate = sem("vec_gate"), sem("act_gate")
        qb_full = sem("qb_full")
        combined = sem("combined")
        vec_att = sem("vec_att")
        mixed = sem("mixed")
        passed = sem("passed")
        mb_full = [sem("mb0_full"), sem("mb1_full")]
        mb_read = [sem("mb0_read"), sem("mb1_read")]

        def wait(eng, s, value):
            if not isinstance(value, int) or value > 0:
                eng.wait_ge(s, value)

        def stand(eng, i=None):
            eng.sem_inc(passed, 1)

        def wait_read(eng, bank, i, what):
            stage = dict(BANK_USES[bank])[what]
            if stage in stages_of(i):
                eng.wait_ge(mb_read[bank], bank_use(bank, i, what))

        def iterations(eng, one):
            for i in (-1, 0, 1):
                one(i)
            with eng.Fori(2, NB - 1) as i:
                one(i)
            for i in (NB - 1, NB, NB + 1):
                one(i)

        def over_tiles(ap):
            return ap.unsqueeze(1).broadcast_to([P, T, ap.shape[1]])

        def over_experts(ap):
            return ap.unsqueeze(2).broadcast_to([P, T, NE])

        NCONST = 9
        block = ctx.enter_context(nc.Block())

        @block.sync
        def _(sp_eng):
            e = sp_eng

            def load_x(b):
                e.dma_start(xt[:], x[b].rearrange("(t p) c -> p t c", p=P)).then_inc(x_loaded, 16)

            load_x(0)
            e.dma_start(wx[:], WxT.rearrange("(h p) k -> p h k", p=P)).then_inc(const_loaded, 16)
            e.dma_start(wdt[0:RANK, :], WdtT).then_inc(const_loaded, 16)
            e.dma_start(wdt[RANK:RANK + 1, :], b_dt).then_inc(const_loaded, 16)
            e.dma_start(negA[:], A_log.rearrange("(h p) n -> p h n", p=P)).then_inc(const_loaded, 16)
            e.dma_start(dskip[:], D_param.broadcast_to([P, D])).then_inc(const_loaded, 16)
            e.dma_start(sgate[:], gates.broadcast_to([P, NE])).then_inc(const_loaded, 16)
            e.dma_start(simf[:], sim.rearrange("(h p) n -> p h n", p=P)).then_inc(const_loaded, 16)
            e.dma_start(wraw[:], Wqkv.rearrange("(h p) n -> p h n", p=P)).then_inc(const_loaded, 16)
            e.dma_start(wo[:], Wo.rearrange("(k p) c -> p k c", p=P)).then_inc(const_loaded, 16)

            def one(i):
                on = stages_of(i)
                if "prepare" in on and (not isinstance(i, int) or i >= 0):
                    wait(e, pool_prep, step(POOL_PREP, "yinit", i))
                    stand(e)
                    load_x(i + 1)
                if "scan" in on:
                    wait_read(e, 0, i - 1, "dtp")
                    wait_read(e, 1, i - 1, "dtp")
                    wait(e, abar_done, i * 2 * NS)
                    e.dma_start(dt[:], dt_next[:]).then_inc(dt_moved, 16)
                    wait_read(e, 1, i - 1, "bc")
                    stand(e)
                    wait(e, v_done, i * NS)
                    e.dma_start(bcur[:], bc_next[:, :, 0:NS]).then_inc(b_moved, 16)
                    wait_read(e, 0, i - 1, "dtT")
                    stand(e)
                    wait_read(e, 1, i - 1, "dtT")
                    e.dma_start(u[:], u_next[:]).then_inc(u_moved, 16)
                    wait(e, read_out, i * 2 * NS)
                    e.dma_start(ccur[:], bc_next[:, :, NS:2 * NS]).then_inc(c_moved, 16)
                if "attend" in on:
                    wait_read(e, 0, i - 1, "op3")
                    e.dma_start(x2b[:], x2a[:]).then_inc(x2b_moved, 16)
                if "project" in on:
                    if "scan" not in on:
                        wait(e, read_out, i * 2 * NS)
                    wait(e, x2b_moved, (i - 1) * 16)
                    wait(e, pool_proj, i - 1)
                    e.dma_start(x2a[:], y[:]).then_inc(x2a_moved, 16)
                if "scan" in on:
                    wait(e, pool_prep, step(POOL_PREP, "yinit", i))
                    wait(e, x2a_moved, i * 16)
                    e.dma_start(y[:], y_next[:]).then_inc(y_moved, 16)
                if "attend" in on:
                    wait_read(e, 0, i, "op3")
                    stand(e)
                    e.dma_start(out[i - 2].rearrange("(t p) c -> p t c", p=P), outt[:]).then_inc(out_stored, 16)

            iterations(e, one)
            e.wait_ge(out_stored, NB * 16)

        @block.gpsimd
        def _(pool):
            g = nc.gpsimd
            g.memset(ident[:], 0.0).then_inc(pool_const, 1)
            g.memset(causal[:], 0.0).then_inc(pool_const, 1)
            g.memset(ones[:], 1.0).then_inc(pool_const, 1)
            g.memset(dtl[:], 1.0).then_inc(pool_const, 1)
            g.memset(restart[:], 1.0).then_inc(pool_const, 1)
            pool.wait_ge(pool_const, 5)
            g.affine_select(out=ident[:], in_=ident[:], compare_op=ALU.not_equal, fill=1.0, base=0,
                            pattern=[[-1, P]], channel_multiplier=1).then_inc(pool_const, 1)
            g.affine_select(out=causal[:], in_=causal[:], compare_op=ALU.is_ge, fill=MASKED, base=0,
                            pattern=[[-1, P]], channel_multiplier=1).then_inc(pool_const, 1)
            g.memset(restart[:, :, 0:1], 0.0).then_inc(pool_const, 1)
            pool.wait_ge(pool_const, 6)
            g.tensor_copy(identb[:], ident[:]).then_inc(pool_const, 1)
            pool.wait_ge(vec_const, 1)
            g.partition_all_reduce(wmax[:, 1:2], wmax[:, 0:1], P, bass.bass_isa.ReduceOp.max).then_inc(pool_wmax, 1)
            pool.wait_ge(const_loaded, NCONST * 16)

            def b_times_u(i, n):
                wait(pool, dbu_full, i * 2 * NS + 2 * (n - 1))
                stand(pool)
                for t in range(T):
                    last = g.tensor_scalar(v[:, n % 2, t, :], u[:, t, :], bcur[:, t, n:n + 1], 1.0,
                                           ALU.mult, ALU.mult)
                last.then_inc(v_done, 1)

            def one(i):
                on = stages_of(i)
                if "scan" in on:
                    wait(pool, b_moved, (i + 1) * 16)
                    wait(pool, u_moved, (i + 1) * 16)
                    b_times_u(i, 0)
                for n in range(NS):
                    if "scan" in on and n + 1 < NS:
                        b_times_u(i, n + 1)
                    if "project" in on and n == 2:
                        wait(pool, vec_proj, step(VEC_PROJ, "nmr", i - 1))
                        if not isinstance(i, int) or i > 1:
                            wait(pool, mb_full[1], bank_use(1, i - 1, "xh"))
                        stand(pool)
                        for t in range(T):
                            last = g.tensor_scalar(xh[:, t, :], x2a[:, t, :], sm2[:, 4, t:t + 1], sm2[:, 5, t:t + 1],
                                                   ALU.mult, ALU.add)
                        last.then_inc(pool_proj, 1)
                    if "prepare" in on and n == 6:
                        wait(pool, vec_prep, step(VEC_PREP, "nmr", i + 1))
                        wait_read(pool, 0, i - 1, "dtT")
                        wait_read(pool, 1, i - 1, "dtT")
                        stand(pool)
                        for t in range(T):
                            last = g.tensor_scalar(xn[:, t, :], xt[:, t, :], sm1[:, 4, t:t + 1], sm1[:, 5, t:t + 1],
                                                   ALU.mult, ALU.add)
                        last.then_inc(pool_prep, 1)
                        wait(pool, pool_prep, step(POOL_PREP, "xn", i + 1))
                        wait(pool, y_moved, (i + 1) * 16)
                        g.tensor_tensor(y_next[:], xn[:], over_tiles(dskip[:]), ALU.mult).then_inc(pool_prep, 1)
                        wait(pool, pool_prep, step(POOL_PREP, "skip", i + 1))
                        g.tensor_tensor(y_next[:], y_next[:], xt[:], ALU.add).then_inc(pool_prep, 1)
                    if "attend" in on and 10 <= n < 10 + T:
                        t = n - 10
                        if t == 0:
                            wait(pool, vec_att, step(VEC_ATT, "rwn", i - 2))
                            wait(pool, mb_read[0], bank_use(0, i, "pv"))
                        if t >= 2:
                            wait(pool, mb_full[1], bank_use(1, i, f"mix{t - 2}"))
                        elif not isinstance(i, int) or i > 2:
                            wait(pool, mb_full[1], bank_use(1, i - 1, f"mix{t + 2}"))
                        g.tensor_tensor(mix[:, t % 2], at[:, t, :].unsqueeze(1).broadcast_to([P, NE, HD]),
                                        rwn[:, t, :].unsqueeze(2).broadcast_to([P, NE, HD]),
                                        ALU.mult).then_inc(mixed, 1)

            iterations(pool, one)

        @block.scalar
        def _(act):
            a = nc.scalar
            a.preload_act_table_set("natural_log_exp_and_others")
            act.wait_ge(const_loaded, NCONST * 16)
            act.wait_ge(vec_const, 3)
            a.activation(snorm[:, 1, :], snorm[:, 0, :], ACT.Sqrt).then_inc(act_const, 1)
            a.activation(negA[:], negA[:], ACT.Exp).then_inc(act_const, 1)
            a.activation(sgate[:], sgate[:], ACT.Exp, scale=-1.0).then_inc(act_const, 1)
            act.wait_ge(vec_const, 5)
            a.activation(whi[:], wraw[:], ACT.Copy, scale=wmax[:, 2:3]).then_inc(act_const, 1)
            act.wait_ge(vec_const, 11)
            a.activation(simhi[:], simf[:], ACT.Copy).then_inc(act_const, 1)

            def decay(i, n):
                for half in range(CH):
                    wait(act, scan_done, i * 2 * NS + 2 * (n - 2) + half + 1)
                    a.activation(abar[:, n % 2, half, :], dt[:, half, :], ACT.Exp,
                                 scale=negA[:, half, n:n + 1]).then_inc(abar_done, 1)

            def empty(i, k, what, dst, src):
                act.wait_ge(mb_full[k], bank_use(k, i, what))
                a.activation(dst, src, ACT.Copy).then_inc(mb_read[k], 1)

            def one(i):
                on = stages_of(i)
                if "scan" in on:
                    wait(act, dt_moved, (i + 1) * 16)
                    decay(i, 0)
                for n in range(NS):
                    if "scan" in on and n + 1 < NS:
                        decay(i, n + 1)
                    if "attend" in on:
                        b = i - 2
                        if n == 0:
                            empty(i, 0, "q", qT[:], mb[0][0:HD, :])
                            empty(i, 1, "k", kT[:], mb[1][0:HD, :])
                        if n in (1, 2):
                            for t in (2 * n - 2, 2 * n - 1):
                                act.wait_ge(vec_att, step(VEC_ATT, f"nb{t}", b))
                                w = (t + 1) * P
                                a.activation(pr[:, t, 0:w], mb[t % 2][:, 0:w], ACT.Exp, bias=nb[:, t:t + 1],
                                             scale=HD ** -0.5, accum_out=rs[:, t:t + 1]).then_inc(mb_read[t % 2], 1)
                        if n == 4:
                            empty(i, 1, "pt0", pt[:, 0, :], mb[1][:])
                        if n == 5:
                            empty(i, 0, "pt1", pt[:, 1, P:L], mb[0][:, 0:L - P])
                            empty(i, 1, "pt23", pt[:, 2:4, 2 * P:L],
                                  mb[1][:].rearrange("p (a c) -> p a c", a=2))
                        if n == 6:
                            wait(act, mixed, b * T)
                            empty(i, 0, "pv", at[:], mb[0][:, 0:T * HD].rearrange("p (t d) -> p t d", t=T))
                        if 11 <= n < 11 + T:
                            t = n - 11
                            if t > 0:
                                act.wait_ge(mb_full[0], bank_use(0, i, f"op{t - 1}"))
                            for k in range(2):
                                empty(i, k, f"mix{t}", mixT[:, 4 * k:4 * k + 4, :],
                                      mb[k][:].rearrange("p (c m) -> p c m", c=4))
                    if "project" in on:
                        b = i - 1
                        if n == 1:
                            act.wait_ge(vec_proj, step(VEC_PROJ, "var", b))
                            a.activation(sm2[:, 1, :], sm2[:, 0, :], ACT.Ln).then_inc(act_proj, 1)
                            act.wait_ge(act_proj, step(ACT_PROJ, "ln", b))
                            a.activation(sm2[:, 2, :], sm2[:, 1, :], ACT.Exp, scale=-0.5).then_inc(act_proj, 1)
                        if n == 2:
                            act.wait_ge(vec_proj, step(VEC_PROJ, "ssc", b))
                            a.activation(sm2[:, 8, :], sm2[:, 7, :], ACT.Ln, scale=2.0 ** 40).then_inc(act_proj, 1)
                            act.wait_ge(act_proj, step(ACT_PROJ, "ln2", b))
                            a.activation(sm2[:, 9, :], sm2[:, 8, :], ACT.Exp, scale=-0.5).then_inc(act_proj, 1)
                        if n == 3:
                            wait(act, qb_full, b * 2 * NE)
                            for k in range(CH):
                                act.wait_ge(mb_full[k], bank_use(k, i, "xh"))
                                a.activation(xhi[:, k, :], mb[k][:], ACT.Copy).then_inc(act_proj, 1)
                        if n == 4:
                            act.wait_ge(vec_gate, step(VEC_GATE, "shift", b))
                            a.activation(ex[:], g1[:, 8], ACT.Exp).then_inc(act_gate, 1)
                    if "prepare" in on:
                        b = i + 1
                        if n == 5:
                            act.wait_ge(vec_prep, step(VEC_PREP, "var", b))
                            a.activation(sm1[:, 1, :], sm1[:, 0, :], ACT.Ln).then_inc(act_prep, 1)
                            act.wait_ge(act_prep, step(ACT_PREP, "ln", b))
                            a.activation(sm1[:, 2, :], sm1[:, 1, :], ACT.Exp, scale=-0.5).then_inc(act_prep, 1)
                        if n == 7:
                            empty(i, 0, "xn", xnT[:, 0, :], mb[0][:])
                            empty(i, 1, "xn", xnT[:, 1, :], mb[1][:])
                        if n == 8:
                            if isinstance(b, int) and b == 0:
                                act.wait_ge(pool_const, 4)
                            empty(i, 0, "dtl", dtl[0:RANK, :], mb[0][0:RANK, :])
                            wait(act, b_moved, b * 16)
                            wait(act, c_moved, b * 16)
                            empty(i, 1, "bc", bc_next[:], mb[1][:, 0:T * 2 * NS].rearrange("p (t k) -> p t k", t=T))
                        if n == 9:
                            for k in range(CH):
                                act.wait_ge(mb_full[k], bank_use(k, i, "dtp"))
                                ins = a.activation(sp[:, k, :], mb[k][:], ACT.Abs)
                            ins.then_inc(act_prep, 1)
                            act.wait_ge(act_prep, step(ACT_PREP, "abs", b))
                            a.activation(sp[:], sp[:], ACT.Exp, scale=-1.0).then_inc(act_prep, 1)
                            act.wait_ge(act_prep, step(ACT_PREP, "exp", b))
                            a.activation(sp[:], sp[:], ACT.Ln, bias=1.0).then_inc(act_prep, 1)

            iterations(act, one)

        @block.vector
        def _(dve):
            w = nc.vector
            dve.wait_ge(const_loaded, NCONST * 16)
            w.tensor_reduce(wmax[:, 0:1], wraw[:], mybir.AxisListType.XY, ALU.max,
                            apply_absolute_value=True).then_inc(vec_const, 1)
            w.tensor_tensor(simsq[:], simf[:], simf[:], ALU.mult).then_inc(vec_const, 1)
            dve.wait_ge(pe_const, 1)
            w.tensor_scalar(snorm[:, 0, :], mb[0][:, 0:NE], NORM_MIN_SQ, None, ALU.max).then_inc(vec_const, 1)
            dve.wait_ge(pool_wmax, 1)
            w.tensor_scalar(wmax[:, 3:4], wmax[:, 1:2], 1.0 / W_TOP, 1e-30, ALU.mult, ALU.max).then_inc(vec_const, 1)
            dve.wait_ge(vec_const, 4)
            w.reciprocal(wmax[:, 2:3], wmax[:, 3:4]).then_inc(vec_const, 1)
            dve.wait_ge(act_const, 1)
            w.reciprocal(snorm[:, 2, :], snorm[:, 1, :]).then_inc(vec_const, 1)
            dve.wait_ge(vec_const, 6)
            w.tensor_tensor(snorm[:, 2, :], snorm[:, 2, :], snorm[:, 0, :], ALU.mult).then_inc(vec_const, 1)
            dve.wait_ge(vec_const, 7)
            w.tensor_tensor(snorm[:, 3, :], snorm[:, 2, :], snorm[:, 1, :], ALU.add).then_inc(vec_const, 1)
            dve.wait_ge(vec_const, 8)
            w.tensor_scalar(snorm[:, 3, :], snorm[:, 3, :], 0.5 / SIM_SCALE, 1e-12 / SIM_SCALE, ALU.mult,
                            ALU.max).then_inc(vec_const, 1)
            dve.wait_ge(vec_const, 9)
            w.reciprocal(snorm[:, 3, :], snorm[:, 3, :]).then_inc(vec_const, 1)
            dve.wait_ge(vec_const, 10)
            w.tensor_tensor(simf[:], simf[:], snorm[:, 3, :].unsqueeze(1).broadcast_to([P, CH, NE]),
                            ALU.mult).then_inc(vec_const, 1)
            dve.wait_ge(act_const, 3)
            w.tensor_scalar(negA[:], negA[:], -1.0, None, ALU.mult).then_inc(vec_const, 1)
            w.tensor_scalar(sgate[:], sgate[:], 1.0, None, ALU.add).then_inc(vec_const, 1)
            dve.wait_ge(vec_const, 13)
            w.reciprocal(sgate[:], sgate[:]).then_inc(vec_const, 1)
            dve.wait_ge(act_const, 4)
            w.scalar_tensor_tensor(out=wlo[:], in0=wraw[:], scalar=wmax[:, 2:3], in1=whi[:], op0=ALU.mult,
                                   op1=ALU.subtract).then_inc(vec_const, 1)
            dve.wait_ge(act_const, 5)
            w.tensor_tensor(simlo[:], simf[:], simhi[:], ALU.subtract).then_inc(vec_const, 1)
            dve.wait_ge(vec_const, 16)
            dve.wait_ge(pool_const, 9)

            def statistics(s, steps, b, src, st, mv, sm):
                for t in range(T):
                    ins = w.bn_stats(st[:, t, :], src[:, t, :])
                ins.then_inc(s, 1)
                dve.wait_ge(s, step(steps, "stats", b))
                stand(dve)
                for t in range(T):
                    ins = w.bn_aggr(mv[:, t, :], st[:, t, :])
                ins.then_inc(s, 1)
                dve.wait_ge(s, step(steps, "aggr", b))
                w.tensor_scalar(sm[:, 0, :], mv[:, :, 1], EPS, None, ALU.add).then_inc(s, 1)

            def newton_rstd(s, steps, b, mv, sm):
                w.tensor_tensor(sm[:, 3, :], sm[:, 2, :], sm[:, 2, :], ALU.mult).then_inc(s, 1)
                dve.wait_ge(s, step(steps, "sq", b))
                w.tensor_tensor(sm[:, 3, :], sm[:, 3, :], sm[:, 0, :], ALU.mult).then_inc(s, 1)
                dve.wait_ge(s, step(steps, "vsq", b))
                w.tensor_scalar(sm[:, 3, :], sm[:, 3, :], -0.5, 1.5, ALU.mult, ALU.add).then_inc(s, 1)
                dve.wait_ge(s, step(steps, "cor", b))
                w.tensor_tensor(sm[:, 4, :], sm[:, 2, :], sm[:, 3, :], ALU.mult).then_inc(s, 1)
                dve.wait_ge(s, step(steps, "rstd", b))
                w.scalar_tensor_tensor(out=sm[:, 5, :], in0=mv[:, :, 0], scalar=-1.0, in1=sm[:, 4, :], op0=ALU.mult,
                                       op1=ALU.mult).then_inc(s, 1)

            def scan(i, n, half):
                dve.wait_ge(abar_done, i * 2 * NS + 2 * n + half + 1)
                dve.wait_ge(dbu_full, i * 2 * NS + 2 * n + half + 1)
                wait(dve, hT_full, i * 2 * NS + 2 * (n - 1))
                w.tensor_tensor_scan(h[:, n % 2, half, :], abar[:, n % 2, half, :], dbu[half][:], 0.0,
                                     ALU.mult, ALU.add).then_inc(scan_done, 1)

            def readout(i, n, k):
                dve.wait_ge(hT_full, i * 2 * NS + 2 * n + k + 1)
                if n == 0 and k == 0:
                    dve.wait_ge(y_moved, (i + 1) * 16)
                    dve.wait_ge(c_moved, (i + 1) * 16)
                if n > 0:
                    dve.wait_ge(read_out, i * 2 * NS + 2 * (n - 1) + k + 1)
                for t in (2 * k, 2 * k + 1):
                    ins = w.scalar_tensor_tensor(out=y[:, t, :], in0=hT[k][:, (t % 2) * D:(t % 2 + 1) * D],
                                                 scalar=ccur[:, t, n:n + 1], in1=y[:, t, :], op0=ALU.mult,
                                                 op1=ALU.add)
                ins.then_inc(read_out, 1)

            def combine(i, e):
                b = i - 1
                if e == 0:
                    dve.wait_ge(vec_gate, step(VEC_GATE, "rws", b))
                if e == NE - 1 and "attend" in stages_of(i):
                    dve.wait_ge(mb_full[0], bank_use(0, i, "pv"))
                for k in range(2):
                    dve.wait_ge(qb_full, b * 2 * NE + 2 * e + k + 1)
                    if e > 0:
                        dve.wait_ge(combined, b * 2 * NE + 2 * (e - 1) + k + 1)
                    for t in (2 * k, 2 * k + 1):
                        src = qb[k][:, (t % 2) * QKV:(t % 2 + 1) * QKV]
                        if e == 0:
                            ins = w.tensor_scalar(acc[:, t, :], src, rws[:, t, e:e + 1], None, ALU.mult)
                        else:
                            dst = qkv if e == NE - 1 else acc
                            ins = w.scalar_tensor_tensor(out=dst[:, t, :], in0=src, scalar=rws[:, t, e:e + 1],
                                                         in1=acc[:, t, :], op0=ALU.mult, op1=ALU.add)
                    ins.then_inc(combined, 1)

            def gating(i):
                b = i - 1
                k = vec_gate

                def at_step(name):
                    dve.wait_ge(k, step(VEC_GATE, name, b))

                dve.wait_ge(vec_proj, step(VEC_PROJ, "r", b))
                dve.wait_ge(mb_full[0], bank_use(0, i, "logit"))
                for t in range(T):
                    ins = w.scalar_tensor_tensor(out=lg[:, t, :], in0=mb[0][:, t * NE:(t + 1) * NE],
                                                 scalar=sm2[:, 13, t:t + 1], in1=sgate[:], op0=ALU.mult,
                                                 op1=ALU.subtract)
                ins.then_inc(mb_read[0], 1)
                dve.wait_ge(mb_read[0], bank_use(0, i, "logit"))
                stand(dve)
                for t in range(T):
                    ins = w.max(top8[:, t, :], lg[:, t, :])
                ins.then_inc(k, 1)
                at_step("top")
                first, second = top8[:, :, 0], top8[:, :, 1]
                w.tensor_tensor(g1[:, 0], lg[:], over_experts(second), ALU.is_gt).then_inc(k, 1)
                w.tensor_tensor(g1[:, 1], lg[:], over_experts(second), ALU.is_equal).then_inc(k, 1)
                at_step("eq")
                w.tensor_tensor_scan(g1[:, 2].rearrange("p t e -> p (t e)"), restart[:].rearrange("p t e -> p (t e)"),
                                     g1[:, 1].rearrange("p t e -> p (t e)"), 0.0, ALU.mult, ALU.add).then_inc(k, 1)
                w.tensor_tensor(gs[:, 0, :], first, second, ALU.is_le).then_inc(k, 1)
                at_step("room")
                w.scalar_tensor_tensor(out=g1[:, 3], in0=g1[:, 2], scalar=-1.0, in1=over_experts(gs[:, 0, :]),
                                       op0=ALU.add, op1=ALU.is_le).then_inc(k, 1)
                at_step("fit")
                w.tensor_tensor(g1[:, 4], g1[:, 3], g1[:, 1], ALU.mult).then_inc(k, 1)
                at_step("take")
                w.tensor_tensor(g1[:, 4], g1[:, 4], g1[:, 0], ALU.add).then_inc(k, 1)
                w.tensor_scalar(gs[:, 1, :], first, 0.0, None, ALU.is_le).then_inc(k, 1)
                at_step("idle")
                w.tensor_tensor(g1[:, 5], g1[:, 4], over_experts(gs[:, 1, :]), ALU.mult).then_inc(k, 1)
                at_step("fbm")
                w.scalar_tensor_tensor(out=g1[:, 6], in0=lg[:], scalar=0.0, in1=g1[:, 5], op0=ALU.is_gt,
                                       op1=ALU.max).then_inc(k, 1)
                w.tensor_scalar(g1[:, 7], lg[:], 0.0, None, ALU.max).then_inc(k, 1)
                w.tensor_scalar(gs[:, 2, :], first, 0.0, None, ALU.max).then_inc(k, 1)
                at_step("gmax")
                w.tensor_tensor(g1[:, 8], g1[:, 7], over_experts(gs[:, 2, :]), ALU.subtract).then_inc(k, 1)
                dve.wait_ge(act_gate, b + 1)
                w.tensor_tensor(g1[:, 9], ex[:], g1[:, 6], ALU.mult).then_inc(k, 1)
                at_step("kept")
                w.tensor_reduce(gs[:, 3, :], g1[:, 9], AX_X, ALU.add).then_inc(k, 1)
                at_step("sum")
                w.reciprocal(gs[:, 4, :], gs[:, 3, :]).then_inc(k, 1)
                at_step("rsum")
                w.tensor_tensor(rw[:], g1[:, 9], over_experts(gs[:, 4, :]), ALU.mult).then_inc(k, 1)
                at_step("rw")
                w.tensor_scalar(rws[:], rw[:], wmax[:, 3:4], None, ALU.mult).then_inc(k, 1)

            def one(i):
                on = stages_of(i)
                for n in range(NS):
                    if "scan" in on:
                        scan(i, n, 0)
                        if n > 0:
                            readout(i, n - 1, 0)
                        scan(i, n, 1)
                        if n > 0:
                            readout(i, n - 1, 1)
                    experts = EXPERTS_AT.get(n, []) if "project" in on else []
                    for e in experts[:1]:
                        combine(i, e)
                    if "attend" in on:
                        b = i - 2
                        if n in (1, 2):
                            for t in (2 * n - 2, 2 * n - 1):
                                dve.wait_ge(mb_full[t % 2], bank_use(t % 2, i, f"s{t}"))
                                w.tensor_reduce(mx[:, t:t + 1], mb[t % 2][:, 0:(t + 1) * P], AX_X,
                                                ALU.max).then_inc(vec_att, 1)
                                dve.wait_ge(vec_att, step(VEC_ATT, f"mx{t}", b))
                                w.tensor_scalar(nb[:, t:t + 1], mx[:, t:t + 1], -(HD ** -0.5), None,
                                                ALU.mult).then_inc(vec_att, 1)
                        if n == 3:
                            dve.wait_ge(mb_read[0], bank_use(0, i, "s2"))
                            dve.wait_ge(mb_read[1], bank_use(1, i, "s3"))
                            w.reciprocal(rinv[:], rs[:]).then_inc(vec_att, 1)
                            dve.wait_ge(vec_att, step(VEC_ATT, "rinv", b))
                            wait(dve, mixed, b * T)
                            w.tensor_tensor(rwn[:], rw[:], over_experts(rinv[:]), ALU.mult).then_inc(vec_att, 1)
                        if n >= 12:
                            t = n - 12
                            if t == 0:
                                wait(dve, out_stored, b * 16)
                                dve.wait_ge(x2b_moved, (b + 1) * 16)
                            dve.wait_ge(mb_full[0], bank_use(0, i, f"op{t}"))
                            w.tensor_tensor(outt[:, t, :], mb[0][:, 0:D], x2b[:, t, :],
                                            ALU.add).then_inc(mb_read[0], 1)
                    if "project" in on:
                        b = i - 1
                        if n == 1:
                            dve.wait_ge(x2a_moved, (b + 1) * 16)
                            statistics(vec_proj, VEC_PROJ, b, x2a, st2, mv2, sm2)
                        if n == 2:
                            dve.wait_ge(act_proj, step(ACT_PROJ, "y0", b))
                            newton_rstd(vec_proj, VEC_PROJ, b, mv2, sm2)
                            w.tensor_tensor(sm2[:, 6, :], sm2[:, 4, :], sm2[:, 4, :], ALU.mult).then_inc(vec_proj, 1)
                            dve.wait_ge(vec_proj, step(VEC_PROJ, "rr", b))
                            w.scalar_tensor_tensor(out=sm2[:, 6, :], in0=sm2[:, 6, :], scalar=float(D),
                                                   in1=mv2[:, :, 1], op0=ALU.mult, op1=ALU.mult).then_inc(vec_proj, 1)
                            dve.wait_ge(vec_proj, step(VEC_PROJ, "ss", b))
                            w.tensor_scalar(sm2[:, 7, :], sm2[:, 6, :], NORM_MIN_SQ, None,
                                            ALU.max).then_inc(vec_proj, 1)
                            dve.wait_ge(act_proj, step(ACT_PROJ, "y2", b))
                            w.tensor_scalar(sm2[:, 10, :], sm2[:, 9, :], 2.0 ** 20, None,
                                            ALU.mult).then_inc(vec_proj, 1)
                            dve.wait_ge(vec_proj, step(VEC_PROJ, "y", b))
                            w.tensor_tensor(sm2[:, 11, :], sm2[:, 10, :], sm2[:, 10, :], ALU.mult).then_inc(vec_proj, 1)
                            dve.wait_ge(vec_proj, step(VEC_PROJ, "ysq", b))
                            w.tensor_tensor(sm2[:, 11, :], sm2[:, 11, :], sm2[:, 7, :], ALU.mult).then_inc(vec_proj, 1)
                            dve.wait_ge(vec_proj, step(VEC_PROJ, "yv", b))
                            w.tensor_scalar(sm2[:, 12, :], sm2[:, 11, :], -0.5, 1.5, ALU.mult,
                                            ALU.add).then_inc(vec_proj, 1)
                            dve.wait_ge(vec_proj, step(VEC_PROJ, "ycor", b))
                            w.scalar_tensor_tensor(out=sm2[:, 13, :], in0=sm2[:, 10, :], scalar=1.0 / SIM_SCALE,
                                                   in1=sm2[:, 12, :], op0=ALU.mult, op1=ALU.mult).then_inc(vec_proj, 1)
                        if n == 3:
                            for k in range(CH):
                                dve.wait_ge(act_proj, step(ACT_PROJ, f"hi{k}", b))
                                w.tensor_tensor(xlo[:, k, :], mb[k][:], xhi[:, k, :],
                                                ALU.subtract).then_inc(mb_read[k], 1)
                        if n == 4:
                            gating(i)
                    if "prepare" in on:
                        b = i + 1
                        if n == 5:
                            dve.wait_ge(x_loaded, (b + 1) * 16)
                            statistics(vec_prep, VEC_PREP, b, xt, st1, mv1, sm1)
                        if n == 6:
                            dve.wait_ge(act_prep, step(ACT_PREP, "y0", b))
                            newton_rstd(vec_prep, VEC_PREP, b, mv1, sm1)
                        if n == 9:
                            dve.wait_ge(act_prep, step(ACT_PREP, "softplus", b))
                            wait(dve, dt_moved, b * 16)
                            for k in range(CH):
                                w.scalar_tensor_tensor(out=dt_next[:, k, :], in0=mb[k][:], scalar=0.0,
                                                       in1=sp[:, k, :], op0=ALU.max,
                                                       op1=ALU.add).then_inc(mb_read[k], 1)
                        if n == 10:
                            wait(dve, u_moved, b * 16)
                            dve.wait_ge(pool_prep, step(POOL_PREP, "xn", b))
                            for k in range(2):
                                dve.wait_ge(mb_full[k], bank_use(k, i, "dtT"))
                                w.tensor_tensor(u_next[:, 2 * k:2 * k + 2, :],
                                                mb[k][:].rearrange("p (t c) -> p t c", t=2),
                                                xn[:, 2 * k:2 * k + 2, :], ALU.mult).then_inc(mb_read[k], 1)
                    for e in experts[1:]:
                        combine(i, e)
                if "scan" in on:
                    readout(i, NS - 1, 0)
                    readout(i, NS - 1, 1)

            iterations(dve, one)

        @block.tensor
        def _(pe):
            m = nc.tensor
            pe.wait_ge(const_loaded, NCONST * 16)
            pe.wait_ge(pool_const, 9)
            pe.wait_ge(vec_const, 2)
            for k in range(CH):
                ins = m.matmul(mb[0][:, 0:NE], ones[:], simsq[:, k, :], start=k == 0, stop=k == CH - 1)
            ins.then_inc(pe_const, 1)
            pe.wait_ge(vec_const, 16)

            def claim(k, i, what):
                wait(pe, mb_read[k], bank_use(k, i, what) - 1)

            def turn_dbu(i, n, half):
                wait(pe, scan_done, i * 2 * NS + 2 * (n - 1) + half + 1)
                for t in range(T):
                    ins = m.transpose(dbu[half][:, t * P:(t + 1) * P], v[:, n % 2, t, half * P:(half + 1) * P],
                                      ident[:])
                ins.then_inc(dbu_full, 1)

            def turn_h(i, n):
                pe.wait_ge(scan_done, i * 2 * NS + 2 * n + 2)
                for k in range(2):
                    wait(pe, read_out, i * 2 * NS + 2 * (n - 1) + k + 1)
                    for t in (2 * k, 2 * k + 1):
                        for half in range(CH):
                            c = (t % 2) * D + half * P
                            ins = m.transpose(hT[k][:, c:c + P], h[:, n % 2, half, t * P:(t + 1) * P], ident[:])
                    ins.then_inc(hT_full, 1)

            def project(i, e):
                b = i - 1
                for k in range(2):
                    wait(pe, combined, b * 2 * NE + 2 * (e - 1) + k + 1)
                    for t in (2 * k, 2 * k + 1):
                        dst = qb[k][:, (t % 2) * QKV:(t % 2 + 1) * QKV]
                        parts = [(s, wt, c) for c in range(CH) for s, wt in ((xhi, whi), (xhi, wlo), (xlo, whi))]
                        for j, (s, wt, c) in enumerate(parts):
                            ins = m.matmul(dst, s[:, c, t * P:(t + 1) * P], wt[:, c, e * QKV:(e + 1) * QKV],
                                           start=j == 0, stop=j == len(parts) - 1)
                    ins.then_inc(qb_full, 1)

            def scores(i, t):
                k = t % 2
                claim(k, i, f"s{t}")
                w = (t + 1) * P
                m.matmul(mb[k][:, 0:w], qT[:, t * P:(t + 1) * P], kT[:, 0:w], start=True, stop=False)
                m.matmul(mb[k][:, t * P:w], identb[:], causal[:], start=False, stop=True).then_inc(mb_full[k], 1)

            def turn_mix(i, t):
                pe.wait_ge(mixed, (i - 2) * T + t + 1)
                for k in range(2):
                    claim(k, i, f"mix{t}")
                    for c in range(4):
                        e = 2 * (4 * k + c)
                        ins = m.transpose(mb[k][:, c * P:(c + 1) * P],
                                          mix[:, t % 2, e:e + 2, :].rearrange("p e d -> p (e d)"), ident[:])
                    ins.then_inc(mb_full[k], 1)

            def out_projection(i, t):
                claim(0, i, f"op{t}")
                pe.wait_ge(mb_read[1], bank_use(1, i, f"mix{t}"))
                for k in range(KO):
                    ins = m.matmul(mb[0][:, 0:D], mixT[:, k, :], wo[:, k, :], start=k == 0, stop=k == KO - 1)
                ins.then_inc(mb_full[0], 1)

            def one(i):
                on = stages_of(i)
                for n in range(NS):
                    if "scan" in on:
                        pe.wait_ge(v_done, i * NS + n + 1)
                        turn_dbu(i, n, 0)
                        if n > 0:
                            turn_h(i, n - 1)
                        turn_dbu(i, n, 1)
                    experts = EXPERTS_AT.get(n, []) if "project" in on else []
                    for e in experts[:1]:
                        project(i, e)
                    if "attend" in on:
                        if n == 0:
                            pe.wait_ge(combined, (i - 1) * 2 * NE)
                            for k in range(2):
                                claim(k, i, "qk"[k])
                                stand(pe)
                                for t in range(T):
                                    ins = m.transpose(mb[k][0:HD, t * P:(t + 1) * P],
                                                      qkv[:, t, k * HD:(k + 1) * HD], ident[:])
                                ins.then_inc(mb_full[k], 1)
                        if n == 1:
                            pe.wait_ge(mb_read[0], bank_use(0, i, "q"))
                            pe.wait_ge(mb_read[1], bank_use(1, i, "k"))
                            scores(i, 0)
                            scores(i, 1)
                        if n == 2:
                            scores(i, 2)
                            scores(i, 3)
                        if n == 4:
                            pe.wait_ge(mb_read[0], bank_use(0, i, "s2"))
                            claim(1, i, "pt0")
                            for t in range(T):
                                ins = m.transpose(mb[1][:, t * P:(t + 1) * P], pr[:, t, 0:P], ident[:])
                            ins.then_inc(mb_full[1], 1)
                    if "project" in on:
                        b = i - 1
                        if n == 3:
                            pe.wait_ge(pool_proj, b + 1)
                            for k in range(CH):
                                claim(k, i, "xh")
                                for t in range(T):
                                    ins = m.transpose(mb[k][:, t * P:(t + 1) * P], xh[:, t, k * P:(k + 1) * P],
                                                      ident[:])
                                ins.then_inc(mb_full[k], 1)
                        if n == 4:
                            claim(0, i, "logit")
                            pe.wait_ge(mb_read[1], bank_use(1, i, "xh"))
                            for t in range(T):
                                parts = [(s, wt, c) for c in range(CH)
                                         for s, wt in ((xhi, simhi), (xhi, simlo), (xlo, simhi))]
                                for j, (s, wt, c) in enumerate(parts):
                                    ins = m.matmul(mb[0][:, t * NE:(t + 1) * NE], s[:, c, t * P:(t + 1) * P],
                                                   wt[:, c, :], start=j == 0, stop=j == len(parts) - 1)
                            ins.then_inc(mb_full[0], 1)
                    if "attend" in on:
                        if n == 5:
                            claim(0, i, "pt1")
                            for t in range(1, T):
                                ins = m.transpose(mb[0][:, (t - 1) * P:t * P], pr[:, t, P:2 * P], ident[:])
                            ins.then_inc(mb_full[0], 1)
                            claim(1, i, "pt23")
                            m.transpose(mb[1][:, 0:P], pr[:, 2, 2 * P:3 * P], ident[:])
                            m.transpose(mb[1][:, P:2 * P], pr[:, 3, 2 * P:3 * P], ident[:])
                            m.transpose(mb[1][:, 2 * P:3 * P], pr[:, 3, 2 * P:3 * P], ident[:])
                            m.transpose(mb[1][:, 3 * P:4 * P], pr[:, 3, 3 * P:4 * P],
                                        ident[:]).then_inc(mb_full[1], 1)
                        if n == 6:
                            claim(0, i, "pv")
                            pe.wait_ge(mb_read[1], bank_use(1, i, "pt23"))
                            for t in range(T):
                                for j in range(t + 1):
                                    ins = m.matmul(mb[0][:, t * HD:(t + 1) * HD], pt[:, j, t * P:(t + 1) * P],
                                                   qkv[:, j, 2 * HD:3 * HD], start=j == 0, stop=j == t)
                            ins.then_inc(mb_full[0], 1)
                    if "prepare" in on:
                        b = i + 1
                        if n == 7:
                            pe.wait_ge(pool_prep, step(POOL_PREP, "xn", b))
                            for k in range(CH):
                                claim(k, i, "xn")
                                for t in range(T):
                                    ins = m.transpose(mb[k][:, t * P:(t + 1) * P], xn[:, t, k * P:(k + 1) * P],
                                                      ident[:])
                                ins.then_inc(mb_full[k], 1)
                        if n == 8:
                            claim(0, i, "dtl")
                            pe.wait_ge(mb_read[1], bank_use(1, i, "xn"))
                            for k in range(CH):
                                ins = m.matmul(mb[0][0:RANK, :], wx[:, k, 0:RANK], xnT[:, k, :], start=k == 0,
                                               stop=k == CH - 1)
                            ins.then_inc(mb_full[0], 1)
                            claim(1, i, "bc")
                            for t in range(T):
                                for k in range(CH):
                                    ins = m.matmul(mb[1][:, t * 2 * NS:(t + 1) * 2 * NS],
                                                   xnT[:, k, t * P:(t + 1) * P], wx[:, k, RANK:RANK + 2 * NS],
                                                   start=k == 0, stop=k == CH - 1)
                            ins.then_inc(mb_full[1], 1)
                        if n == 9:
                            for k in range(CH):
                                claim(k, i, "dtp")
                                m.matmul(mb[k][:], wdt[:, k * P:(k + 1) * P], dtl[:], start=True,
                                         stop=True).then_inc(mb_full[k], 1)
                        if n == 10:
                            claim(0, i, "dtT")
                            claim(1, i, "dtT")
                            for k in range(2):
                                for t in (2 * k, 2 * k + 1):
                                    for half in range(CH):
                                        c = (t % 2) * D + half * P
                                        ins = m.transpose(mb[k][:, c:c + P], dt_next[:, half, t * P:(t + 1) * P],
                                                          ident[:])
                                ins.then_inc(mb_full[k], 1)
                    if "attend" in on:
                        if n >= 12:
                            out_projection(i, n - 12)
                        if 11 <= n < 11 + T:
                            turn_mix(i, n - 11)
                    for e in experts[1:]:
                        project(i, e)
                if "scan" in on:
                    turn_h(i, NS - 1)

            iterations(pe, one)


_OUT = (NB, L, D)


def kernel(**inputs):
    import numpy as np
    import concourse.bacc as bacc
    from concourse.bass_utils import run_bass_kernel_spmd

    def take(name):
        return np.asarray(inputs[name])

    arrays = {
        "x": take("L0_attn_x"),
        "A_log": take("L0_attn_A_log"),
        "D_param": take("L0_attn_D_param").reshape(1, D),
        "WxT": take("L0_attn_W_x").T,
        "WdtT": take("L0_attn_W_dt").T,
        "b_dt": take("L0_attn_b_dt").reshape(1, D),
        "sim": take("L0_ffn_sim_matrix"),
        "gates": take("L0_ffn_gates").reshape(1, NE),
        "Wqkv": np.stack([take(f"L0_ffn_{n}_proj") for n in "qkv"], 2).transpose(1, 0, 2, 3).reshape(D, NE * QKV),
        "Wo": take("L0_ffn_o_proj").reshape(NE * HD, D),
    }
    arrays = {k: np.ascontiguousarray(a) for k, a in arrays.items()}
    nc = bacc.Bacc("TRN2", target_bir_lowering=False, num_devices=1)
    args = [nc.dram_tensor(f"{k}_dram", a.shape, mybir.dt.from_np(a.dtype), kind="ExternalInput").ap()
            for k, a in arrays.items()]
    args.append(nc.dram_tensor("out_dram", _OUT, F32, kind="ExternalOutput").ap())
    scan_attention_kernel(nc, *args)
    r = run_bass_kernel_spmd(nc, [{f"{k}_dram": a for k, a in arrays.items()}], core_ids=[0])
    return r.results[0]["out_dram"]
```

```python
from contextlib import ExitStack

import concourse.bass as bass
from concourse import mybir

ALU = mybir.AluOpType
ACT = mybir.ActivationFunctionType
F32 = mybir.dt.float32
F16 = mybir.dt.float16
BF16 = mybir.dt.bfloat16
AX_X = mybir.AxisListType.X

P = 128
NB, L, D = 16, 512, 256
NS, RANK = 16, 64
NE, HD = 16, 64
T = L // P
CH = D // P
QKV = 3 * HD
KO = NE * HD // P
EPS = 1e-5
NORM_MIN_SQ = 1e-24
SIM_SCALE = 64.0
W_TOP = 256.0
MASKED = -1e30
BG = 4

EXPERTS_AT = {5: [0], 6: [1], 7: [2, 3], 8: [4], 9: [5], 10: [6, 7], 11: [8], 12: [9, 10], 13: [11, 12], 14: [13, 14],
              15: [15]}
OUT_AT = {1: 0, 2: 1, 4: 2, 5: 3}
TURN_AT = {0: 0, 1: 1, 3: 2, 4: 3}

BANK_USES = (
    [("mix0", "output"), ("mix1", "output"), ("xh", "project"), ("mix2", "output"), ("mix3", "output"),
     ("q", "attend"), ("s0", "attend"), ("xn", "prepare"), ("s2", "attend"), ("dtl", "prepare"), ("pt1", "attend"),
     ("dtp", "prepare"), ("pt23", "attend"), ("pv", "attend")],
    [("mix0", "output"), ("mix1", "output"), ("xh", "project"), ("mix2", "output"), ("mix3", "output"),
     ("k", "attend"), ("s1", "attend"), ("xn", "prepare"), ("s3", "attend"), ("c", "prepare"), ("pt0", "attend"),
     ("dtp", "prepare")],
    [("op0", "output"), ("logit", "project"), ("op2", "output")] + [(f"e{e}", "project") for e in range(NE)],
    [("op1", "output"), ("op3", "output")] + [(f"e{e}", "project") for e in range(NE)],
)


def stages_of(i):
    if not isinstance(i, int):
        return {"prepare", "scan", "project", "attend", "output"}
    lag = {"prepare": -1, "scan": 0, "project": 1, "attend": 2, "output": 3}
    return {stage for stage, d in lag.items() if 0 <= i - d < NB}


def bank_use(bank, i, what):
    uses = BANK_USES[bank]
    lag = {"prepare": -1, "project": 1, "attend": 2, "output": 3}
    per = {s: sum(1 for _, stage in uses if stage == s) for s in lag}
    on = stages_of(i)
    inside = 0
    for name, stage in uses:
        if stage in on:
            inside += 1
        if name == what:
            break
    if isinstance(i, int):
        return inside + sum(per[s] * min(max(i - lag[s], 0), NB) for s in lag)
    return i * len(uses) + (inside - sum(per[s] * lag[s] for s in lag))


VEC_PREP = ["stats", "aggr", "var", "sq", "vsq", "cor", "rstd", "nmr"]
ACT_PREP = ["ln", "y0", "abs", "exp", "softplus"]
POOL_PREP = ["xn", "skip", "yinit", "u"]
VEC_PROJ = ["stats", "aggr", "var", "sq", "vsq", "cor", "rstd", "nmr", "rr", "ss", "ssc", "y", "ysq", "yv",
            "ycor", "r"]
ACT_PROJ = ["ln", "y0", "ln2", "y2", "hi0", "hi1"]
VEC_GATE = ["top", "strict", "eq", "rank", "room", "fit", "take", "fb", "idle", "fbm", "mask", "gated", "gmax",
            "shift", "kept", "sum", "rsum", "rw", "rws"]
VEC_ATT = ["rwb", "mx0", "nb0", "mx1", "nb1", "mx2", "nb2", "mx3", "nb3", "rinv", "rwn"]


READS = NS + NS // 2
SCALES = NS // 2


def read_by_vector(b, n, k):
    return b * READS + (n // 2 * 3 + (3 if n % 2 else k + 1))


def step(steps, name, b):
    return b * len(steps) + (steps.index(name) + 1)


def scan_attention_kernel(nc, x, A_log, D_param, WxT, WdtT, b_dt, sim, gates, Wqkv, Wo, b_rows, out):
    with ExitStack() as ctx:
        def sb(name, shape, dt=F32):
            return ctx.enter_context(nc.sbuf_tensor(name, shape, dt))

        def bank(name):
            return ctx.enter_context(nc.psum_tensor(name, [P, 512], F32))

        def sem(name):
            return ctx.enter_context(nc.semaphore(name))

        ident = sb("ident", [P, P])
        identb = sb("identb", [P, P], BF16)
        causal = sb("causal", [P, P], BF16)
        ones = sb("ones", [P, P])
        restart = sb("restart", [P, T, NE])
        wx = sb("wx", [P, CH, RANK + 2 * NS])
        wdt = sb("wdt", [RANK + NS + 1, D])
        negA = sb("negA", [P, CH, NS])
        dskip = sb("dskip", [P, D])
        sgate = sb("sgate", [P, NE])
        simf = sb("simf", [P, CH, NE])
        simsq = sb("simsq", [P, CH, NE])
        simhi = sb("simhi", [P, CH, NE], F16)
        simlo = sb("simlo", [P, CH, NE], F16)
        snorm = sb("snorm", [P, 4, NE])
        wmax = sb("wmax", [P, 4])
        whi = sb("whi", [P, CH, NE * QKV], F16)
        wlo = sb("wlo", [P, CH, NE * QKV], F16)
        wo = sb("wo", [P, KO, D])
        xt = sb("xt", [P, T, D])
        xn = sb("xn", [P, T, D])
        xnT = sb("xnT", [P, CH, L])
        dtl = sb("dtl", [RANK + NS + 1, L])
        sp = sb("sp", [P, CH, L])
        dt_next = sb("dt_next", [P, CH, L])
        u_next = sb("u_next", [P, CH, L])
        y_next = sb("y_next", [P, T, D])
        c_next = sb("c_next", [P, T, NS])
        st1 = sb("st1", [P, T, 6])
        mv1 = sb("mv1", [P, T, 2])
        sm1 = sb("sm1", [P, 6, T])
        dt = sb("dt", [P, CH, L])
        u = sb("u", [P, CH, L])
        y = sb("y", [P, T, D])
        ccur = sb("ccur", [P, T, NS])
        bb = sb("bb", [P, NS, L])
        wraw = bb[:].rearrange("p n l -> p (n l)")[:, 0:CH * NE * QKV].rearrange("p (h c) -> p h c", h=CH)
        v = sb("v", [P, 2, CH, L])
        ytmp = sb("ytmp", [P, 2, 2, D])
        yodd = sb("yodd", [P, 2, D])
        h = sb("h", [P, 2, CH, L])
        x2a = sb("x2a", [P, T, D])
        xh = sb("xh", [P, T, D])
        xhi = sb("xhi", [P, CH, L], F16)
        xlo = sb("xlo", [P, CH, L], F16)
        st2 = sb("st2", [P, T, 6])
        mv2 = sb("mv2", [P, T, 2])
        sm2 = sb("sm2", [P, 14, T])
        lg = sb("lg", [P, T, NE])
        top8 = sb("top8", [P, T, 8])
        g1 = sb("g1", [P, 10, T, NE])
        gs = sb("gs", [P, 6, T])
        ex = sb("ex", [P, T, NE])
        rw = sb("rw", [P, T, NE])
        rws = sb("rws", [P, T, NE])
        acc = sb("acc", [P, T, QKV])
        qkv = sb("qkv", [P, T, QKV])
        x2b = sb("x2b", [P, T, D])
        x2c = sb("x2c", [P, T, D])
        rwb = sb("rwb", [P, T, NE])
        qT = sb("qT", [HD, L])
        kT = sb("kT", [HD, L])
        mx = sb("mx", [P, T])
        nb = sb("nb", [P, T])
        rs = sb("rs", [P, T])
        rinv = sb("rinv", [P, T])
        rwn = sb("rwn", [P, T, NE])
        pr = sb("pr", [P, T, L])
        pt = sb("pt", [P, T, L])
        at = sb("at", [P, T, HD])
        mix = sb("mix", [P, 2, NE, HD])
        mixT = sb("mixT", [P, KO, P])
        outt = sb("outt", [P, T, D])

        ab = [bank("ab0"), bank("ab1")]
        hT = [bank("hT0"), bank("hT1")]
        mb = [bank(f"mb{k}") for k in range(4)]

        const_loaded = sem("const_loaded")
        pool_const = sem("pool_const")
        pool_wmax = sem("pool_wmax")
        vec_const, vec_wdt = sem("vec_const"), sem("vec_wdt")
        act_const = sem("act_const")
        pe_const = sem("pe_const")
        x_loaded = sem("x_loaded")
        dt_moved, u_moved, c_moved = sem("dt_moved"), sem("u_moved"), sem("c_moved")
        b_kept, b_spread = sem("b_kept"), [sem(f"b_spread{g}") for g in range(NS // BG)]
        x2b_moved, x2c_moved = sem("x2b_moved"), sem("x2c_moved")
        out_stored = sem("out_stored")
        vec_prep, act_prep, pool_prep = sem("vec_prep"), sem("act_prep"), sem("pool_prep")
        v_done = sem("v_done")
        abar_done = sem("abar_done")
        scan_done = sem("scan_done")
        hT_full = sem("hT_full")
        read_out = sem("read_out")
        scaled_c, added_c = sem("scaled_c"), sem("added_c")
        vec_proj, act_proj, pool_proj = sem("vec_proj"), sem("act_proj"), sem("pool_proj")
        vec_gate, act_gate = sem("vec_gate"), sem("act_gate")
        vec_att = sem("vec_att")
        mixed = sem("mixed")
        passed = sem("passed")
        mb_full = [sem(f"mb{k}_full") for k in range(4)]
        mb_read = [sem(f"mb{k}_read") for k in range(4)]

        def wait(eng, s, value):
            if not isinstance(value, int) or value > 0:
                eng.wait_ge(s, value)

        def stand(eng, i=None):
            eng.sem_inc(passed, 1)

        def wait_read(eng, bank, i, what):
            stage = dict(BANK_USES[bank])[what]
            if stage in stages_of(i):
                eng.wait_ge(mb_read[bank], bank_use(bank, i, what))

        def iterations(eng, one):
            for i in range(-1, 4):
                one(i)
            with eng.Fori(4, NB - 1) as i:
                one(i)
            for i in range(NB - 1, NB + 3):
                one(i)

        def over_tiles(ap):
            return ap.unsqueeze(1).broadcast_to([P, T, ap.shape[1]])

        def over_experts(ap):
            return ap.unsqueeze(2).broadcast_to([P, T, NE])

        NCONST = 9
        block = ctx.enter_context(nc.Block())

        @block.sync
        def _(sp_eng):
            e = sp_eng

            def load_x(b):
                e.dma_start(xt[:], x[b].rearrange("(t p) c -> p t c", p=P)).then_inc(x_loaded, 16)

            load_x(0)
            e.dma_start(wx[:], WxT.rearrange("(h p) k -> p h k", p=P)).then_inc(const_loaded, 16)
            e.wait_ge(vec_wdt, 1)
            e.dma_start(wdt[0:RANK, :], WdtT).then_inc(const_loaded, 16)
            e.dma_start(wdt[RANK + NS:RANK + NS + 1, :], b_dt).then_inc(const_loaded, 16)
            e.dma_start(negA[:], A_log.rearrange("(h p) n -> p h n", p=P)).then_inc(const_loaded, 16)
            e.dma_start(dskip[:], D_param.broadcast_to([P, D])).then_inc(const_loaded, 16)
            e.dma_start(sgate[:], gates.broadcast_to([P, NE])).then_inc(const_loaded, 16)
            e.dma_start(simf[:], sim.rearrange("(h p) n -> p h n", p=P)).then_inc(const_loaded, 16)
            e.dma_start(wraw, Wqkv.rearrange("(h p) n -> p h n", p=P)).then_inc(const_loaded, 16)
            e.dma_start(wo[:], Wo.rearrange("(k p) c -> p k c", p=P)).then_inc(const_loaded, 16)

            def one(i):
                on = stages_of(i)
                if "scan" in on:
                    wait_read(e, 0, i - 1, "dtp")
                    stand(e)
                    wait_read(e, 1, i - 1, "dtp")
                    stand(e)
                    wait(e, abar_done, i * 2 * NS)
                    e.dma_start(dt[:], dt_next[:]).then_inc(dt_moved, 16)
                    wait(e, pool_prep, step(POOL_PREP, "u", i))
                    stand(e)
                    wait(e, v_done, i * NS)
                    e.dma_start(u[:], u_next[:]).then_inc(u_moved, 16)
                if "prepare" in on and (not isinstance(i, int) or i >= 0):
                    wait(e, pool_prep, step(POOL_PREP, "yinit", i))
                    stand(e)
                    load_x(i + 1)
                if "scan" in on:
                    wait_read(e, 1, i - 1, "c")
                    stand(e)
                    wait(e, read_out, i * READS)
                    stand(e)
                    wait(e, scaled_c, i * SCALES)
                    e.dma_start(ccur[:], c_next[:]).then_inc(c_moved, 16)
                if "output" in on:
                    wait_read(e, 2, i, "op2")
                    stand(e)
                    wait_read(e, 3, i, "op3")
                    stand(e)
                    e.dma_start(out[i - 3].rearrange("(t p) c -> p t c", p=P), outt[:]).then_inc(out_stored, 16)
                if "attend" in on:
                    wait(e, x2b_moved, (i - 1) * 16)
                    e.dma_start(x2c[:], x2b[:]).then_inc(x2c_moved, 16)
                if "project" in on:
                    wait(e, read_out, i * READS)
                    stand(e)
                    wait(e, added_c, i * SCALES)
                    stand(e)
                    wait(e, x2c_moved, (i - 1) * 16)
                    e.dma_start(x2b[:], x2a[:]).then_inc(x2b_moved, 16)
                if "prepare" in on:
                    wait_read(e, 0, i, "dtl")
                    stand(e)
                    for g in range(NS // BG):
                        wait(e, b_spread[g], (i + 1) * 16)
                        stand(e)
                    e.dma_start(b_rows, dtl[RANK:RANK + NS, :]).then_inc(b_kept, 16)
                    wait(e, b_kept, (i + 2) * 16)
                    if isinstance(i, int) and i == -1:
                        e.wait_ge(vec_const, 16)
                    for g in range(NS // BG):
                        if "scan" in on:
                            stand(e)
                            wait(e, v_done, i * NS + BG * (g + 1))
                        e.dma_start(bb[:, g * BG:(g + 1) * BG, :],
                                    b_rows[g * BG:(g + 1) * BG, :].partition_broadcast(P)).then_inc(b_spread[g], 16)

            iterations(e, one)
            e.wait_ge(out_stored, NB * 16)

        @block.gpsimd
        def _(pool):
            g = nc.gpsimd
            g.memset(ident[:], 0.0).then_inc(pool_const, 1)
            g.memset(causal[:], 0.0).then_inc(pool_const, 1)
            g.memset(ones[:], 1.0).then_inc(pool_const, 1)
            g.memset(dtl[:], 1.0).then_inc(pool_const, 1)
            g.memset(restart[:], 1.0).then_inc(pool_const, 1)
            pool.wait_ge(pool_const, 5)
            g.affine_select(out=ident[:], in_=ident[:], compare_op=ALU.not_equal, fill=1.0, base=0,
                            pattern=[[-1, P]], channel_multiplier=1).then_inc(pool_const, 1)
            g.affine_select(out=causal[:], in_=causal[:], compare_op=ALU.is_ge, fill=MASKED, base=0,
                            pattern=[[-1, P]], channel_multiplier=1).then_inc(pool_const, 1)
            g.memset(restart[:, :, 0:1], 0.0).then_inc(pool_const, 1)
            pool.wait_ge(pool_const, 6)
            g.tensor_copy(identb[:], ident[:]).then_inc(pool_const, 1)
            pool.wait_ge(vec_const, 1)
            g.partition_all_reduce(wmax[:, 1:2], wmax[:, 0:1], P, bass.bass_isa.ReduceOp.max).then_inc(pool_wmax, 1)
            pool.wait_ge(const_loaded, NCONST * 16)

            def b_times_u(i, n):
                if n % BG == 0:
                    pool.wait_ge(b_spread[n // BG], (i + 1) * 16)
                wait(pool, scan_done, i * 2 * NS + 2 * (n - 1))
                g.tensor_tensor(v[:, n % 2], u[:], bb[:, n, :].unsqueeze(1).broadcast_to([P, CH, L]),
                                ALU.mult).then_inc(v_done, 1)

            def add_c(i, n):
                wait(pool, scaled_c, i * SCALES + n // 2 + 1)
                if n > 3:
                    stand(pool)
                    wait(pool, added_c, i * SCALES + n // 2 - 1)
                g.tensor_tensor(yodd[:], yodd[:], ytmp[:, n // 2 % 2], ALU.add).then_inc(added_c, 1)

            def join_sums(i):
                wait(pool, added_c, i * SCALES + SCALES - 1)
                stand(pool)
                wait(pool, read_out, read_by_vector(i, NS - 2, 1))
                if not isinstance(i, int) or i > 0:
                    stand(pool)
                    pool.wait_ge(vec_proj, step(VEC_PROJ, "stats", i - 1))
                    stand(pool)
                    pool.wait_ge(x2b_moved, i * 16)
                g.tensor_tensor(x2a[:, 2:4, :], yodd[:], y[:, 2:4, :], ALU.add).then_inc(added_c, 1)

            def mix_heads(i, b, t):
                if t >= 2:
                    wait(pool, mb_full[1], bank_use(1, i, f"mix{t - 2}"))
                elif not isinstance(i, int) or i > 2:
                    wait(pool, mb_full[1], bank_use(1, i, f"mix{t + 2}"))
                g.tensor_tensor(mix[:, t % 2], at[:, t, :].unsqueeze(1).broadcast_to([P, NE, HD]),
                                rwn[:, t, :].unsqueeze(2).broadcast_to([P, NE, HD]),
                                ALU.mult).then_inc(mixed, 1)

            def one(i):
                on = stages_of(i)
                if "scan" in on:
                    wait(pool, u_moved, (i + 1) * 16)
                    b_times_u(i, 0)
                for n in range(NS):
                    if "scan" in on:
                        if n + 1 < NS:
                            b_times_u(i, n + 1)
                        if n > 3 and n % 2 == 0:
                            add_c(i, n - 1)
                    if "output" in on and n in (1, 2):
                        mix_heads(i, i - 3, n + 1)
                    if "project" in on and n == 1:
                        wait(pool, vec_proj, step(VEC_PROJ, "nmr", i - 1))
                        stand(pool)
                        if not isinstance(i, int) or i > 1:
                            wait(pool, mb_full[1], bank_use(1, i - 1, "xh"))
                        stand(pool)
                        for t in range(T):
                            last = g.tensor_scalar(xh[:, t, :], x2a[:, t, :], sm2[:, 4, t:t + 1], sm2[:, 5, t:t + 1],
                                                   ALU.mult, ALU.add)
                        last.then_inc(pool_proj, 1)
                    if "prepare" in on and n == 5:
                        wait(pool, vec_prep, step(VEC_PREP, "nmr", i + 1))
                        stand(pool)
                        if not isinstance(i, int) or i > -1:
                            wait(pool, mb_full[1], bank_use(1, i - 1, "xn"))
                        stand(pool)
                        for t in range(T):
                            last = g.tensor_scalar(xn[:, t, :], xt[:, t, :], sm1[:, 4, t:t + 1], sm1[:, 5, t:t + 1],
                                                   ALU.mult, ALU.add)
                        last.then_inc(pool_prep, 1)
                    if "prepare" in on and n == 7:
                        wait(pool, pool_prep, step(POOL_PREP, "xn", i + 1))
                        if "scan" in on:
                            stand(pool)
                            wait(pool, read_out, read_by_vector(i, 0, 1))
                        g.tensor_tensor(y_next[:], xn[:], over_tiles(dskip[:]), ALU.mult).then_inc(pool_prep, 1)
                        wait(pool, pool_prep, step(POOL_PREP, "skip", i + 1))
                        g.tensor_tensor(y_next[:], y_next[:], xt[:], ALU.add).then_inc(pool_prep, 1)
                    if "prepare" in on and n == 12:
                        wait_read(pool, 0, i, "dtp")
                        stand(pool)
                        wait_read(pool, 1, i, "dtp")
                        if "scan" in on:
                            stand(pool)
                            wait(pool, u_moved, (i + 1) * 16)
                        g.tensor_tensor(u_next[:], dt_next[:], xnT[:], ALU.mult).then_inc(pool_prep, 1)
                    if "attend" in on and n in (14, 15):
                        if n == 14:
                            wait(pool, vec_att, step(VEC_ATT, "rwn", i - 2))
                            stand(pool)
                            wait_read(pool, 0, i, "pv")
                        mix_heads(i, i - 2, n - 14)
                if "scan" in on:
                    add_c(i, NS - 1)
                    join_sums(i)

            iterations(pool, one)

        @block.scalar
        def _(act):
            a = nc.scalar
            act.wait_ge(const_loaded, NCONST * 16)
            act.wait_ge(vec_const, 3)
            a.activation(snorm[:, 1, :], snorm[:, 0, :], ACT.Sqrt).then_inc(act_const, 1)
            a.preload_act_table_set("natural_log_exp_and_others")
            a.activation(negA[:], negA[:], ACT.Exp).then_inc(act_const, 1)
            a.activation(sgate[:], sgate[:], ACT.Exp, scale=-1.0).then_inc(act_const, 1)
            act.wait_ge(vec_const, 5)
            a.activation(whi[:], wraw, ACT.Copy, scale=wmax[:, 2:3]).then_inc(act_const, 1)
            act.wait_ge(vec_const, 11)
            a.activation(simhi[:], simf[:], ACT.Copy).then_inc(act_const, 1)

            def decay(i, n, half):
                wait(act, scan_done, i * 2 * NS + 2 * (n - 1) + half + 1)
                a.activation(ab[half][:], dt[:, half, :], ACT.Exp,
                             scale=negA[:, half, n:n + 1]).then_inc(abar_done, 1)

            def scale_c(i, n):
                act.wait_ge(hT_full, i * 2 * NS + 2 * n + 2)
                if n == 1:
                    act.wait_ge(c_moved, (i + 1) * 16)
                    wait(act, added_c, i * SCALES)
                    dst = yodd
                else:
                    wait(act, added_c, i * SCALES + n // 2 - 2)
                    dst = ytmp[:, n // 2 % 2]
                for t in (2, 3):
                    ins = a.activation(dst[:, t - 2, :], hT[1][:, (t - 2) * D:(t - 1) * D], ACT.Copy,
                                       scale=ccur[:, t, n:n + 1])
                ins.then_inc(scaled_c, 1)

            def empty(i, k, what, dst, src):
                act.wait_ge(mb_full[k], bank_use(k, i, what))
                a.activation(dst, src, ACT.Copy).then_inc(mb_read[k], 1)

            def one(i):
                on = stages_of(i)
                if "scan" in on:
                    wait(act, dt_moved, (i + 1) * 16)
                    decay(i, 0, 0)
                    decay(i, 0, 1)
                for n in range(NS):
                    if "scan" in on:
                        if n + 1 < NS:
                            decay(i, n + 1, 0)
                        if n > 0 and n % 2 == 0:
                            scale_c(i, n - 1)
                        if n + 1 < NS:
                            decay(i, n + 1, 1)
                    if "output" in on and n in TURN_AT:
                        t = TURN_AT[n]
                        if t > 0:
                            k = 2 + (t - 1) % 2
                            act.wait_ge(mb_full[k], bank_use(k, i, f"op{t - 1}"))
                        for k in range(2):
                            empty(i, k, f"mix{t}", mixT[:, 4 * k:4 * k + 4, :],
                                  mb[k][:].rearrange("p (c m) -> p c m", c=4))
                    if "attend" in on:
                        b = i - 2
                        if n == 5:
                            empty(i, 0, "q", qT[:], mb[0][0:HD, :])
                            empty(i, 1, "k", kT[:], mb[1][0:HD, :])
                        if n in (6, 8):
                            for t in (n - 6, n - 5):
                                act.wait_ge(vec_att, step(VEC_ATT, f"nb{t}", b))
                                w = (t + 1) * P
                                a.activation(pr[:, t, 0:w], mb[t % 2][:, 0:w], ACT.Exp, bias=nb[:, t:t + 1],
                                             scale=HD ** -0.5, accum_out=rs[:, t:t + 1]).then_inc(mb_read[t % 2], 1)
                        if n == 10:
                            empty(i, 0, "pt1", pt[:, 1, P:L], mb[0][:, 0:L - P])
                            empty(i, 1, "pt0", pt[:, 0, :], mb[1][:])
                        if n == 12:
                            empty(i, 0, "pt23", pt[:, 2:4, 2 * P:L], mb[0][:].rearrange("p (a c) -> p a c", a=2))
                        if n == 13:
                            wait(act, mixed, b * T)
                            empty(i, 0, "pv", at[:], mb[0][:, 0:T * HD].rearrange("p (t d) -> p t d", t=T))
                    if "project" in on:
                        b = i - 1
                        if n == 0:
                            act.wait_ge(vec_proj, step(VEC_PROJ, "var", b))
                            a.activation(sm2[:, 1, :], sm2[:, 0, :], ACT.Ln).then_inc(act_proj, 1)
                            act.wait_ge(act_proj, step(ACT_PROJ, "ln", b))
                            a.activation(sm2[:, 2, :], sm2[:, 1, :], ACT.Exp, scale=-0.5).then_inc(act_proj, 1)
                        if n == 1:
                            act.wait_ge(vec_proj, step(VEC_PROJ, "ssc", b))
                            a.activation(sm2[:, 8, :], sm2[:, 7, :], ACT.Ln, scale=2.0 ** 40).then_inc(act_proj, 1)
                            act.wait_ge(act_proj, step(ACT_PROJ, "ln2", b))
                            a.activation(sm2[:, 9, :], sm2[:, 8, :], ACT.Exp, scale=-0.5).then_inc(act_proj, 1)
                        if n == 2:
                            for k in range(CH):
                                act.wait_ge(mb_full[k], bank_use(k, i, "xh"))
                                a.activation(xhi[:, k, :], mb[k][:], ACT.Copy).then_inc(act_proj, 1)
                        if n == 3:
                            act.wait_ge(vec_gate, step(VEC_GATE, "shift", b))
                            a.activation(ex[:], g1[:, 8], ACT.Exp).then_inc(act_gate, 1)
                    if "prepare" in on:
                        b = i + 1
                        if n == 4:
                            act.wait_ge(vec_prep, step(VEC_PREP, "var", b))
                            a.activation(sm1[:, 1, :], sm1[:, 0, :], ACT.Ln).then_inc(act_prep, 1)
                            act.wait_ge(act_prep, step(ACT_PREP, "ln", b))
                            a.activation(sm1[:, 2, :], sm1[:, 1, :], ACT.Exp, scale=-0.5).then_inc(act_prep, 1)
                        if n == 7:
                            wait(act, pool_prep, step(POOL_PREP, "u", i))
                            empty(i, 0, "xn", xnT[:, 0, :], mb[0][:])
                            empty(i, 1, "xn", xnT[:, 1, :], mb[1][:])
                        if n == 9:
                            if isinstance(b, int) and b == 0:
                                act.wait_ge(pool_const, 4)
                            wait(act, b_kept, b * 16)
                            empty(i, 0, "dtl", dtl[0:RANK + NS, :], mb[0][0:RANK + NS, :])
                            wait(act, c_moved, b * 16)
                            empty(i, 1, "c", c_next[:], mb[1][:, 0:T * NS].rearrange("p (t k) -> p t k", t=T))
                        if n == 11:
                            for k in range(CH):
                                act.wait_ge(mb_full[k], bank_use(k, i, "dtp"))
                                ins = a.activation(sp[:, k, :], mb[k][:], ACT.Abs)
                            ins.then_inc(act_prep, 1)
                            act.wait_ge(act_prep, step(ACT_PREP, "abs", b))
                            a.activation(sp[:], sp[:], ACT.Exp, scale=-1.0).then_inc(act_prep, 1)
                            act.wait_ge(act_prep, step(ACT_PREP, "exp", b))
                            a.activation(sp[:], sp[:], ACT.Ln, bias=1.0).then_inc(act_prep, 1)
                if "scan" in on:
                    scale_c(i, NS - 1)

            iterations(act, one)

        @block.vector
        def _(dve):
            w = nc.vector
            w.memset(wdt[:], 0.0).then_inc(vec_wdt, 1)
            dve.wait_ge(const_loaded, NCONST * 16)
            w.tensor_reduce(wmax[:, 0:1], wraw, mybir.AxisListType.XY, ALU.max,
                            apply_absolute_value=True).then_inc(vec_const, 1)
            w.tensor_tensor(simsq[:], simf[:], simf[:], ALU.mult).then_inc(vec_const, 1)
            dve.wait_ge(pe_const, 1)
            w.tensor_scalar(snorm[:, 0, :], mb[0][:, 0:NE], NORM_MIN_SQ, None, ALU.max).then_inc(vec_const, 1)
            dve.wait_ge(pool_wmax, 1)
            w.tensor_scalar(wmax[:, 3:4], wmax[:, 1:2], 1.0 / W_TOP, 1e-30, ALU.mult, ALU.max).then_inc(vec_const, 1)
            dve.wait_ge(vec_const, 4)
            w.reciprocal(wmax[:, 2:3], wmax[:, 3:4]).then_inc(vec_const, 1)
            dve.wait_ge(act_const, 1)
            w.reciprocal(snorm[:, 2, :], snorm[:, 1, :]).then_inc(vec_const, 1)
            dve.wait_ge(vec_const, 6)
            w.tensor_tensor(snorm[:, 2, :], snorm[:, 2, :], snorm[:, 0, :], ALU.mult).then_inc(vec_const, 1)
            dve.wait_ge(vec_const, 7)
            w.tensor_tensor(snorm[:, 3, :], snorm[:, 2, :], snorm[:, 1, :], ALU.add).then_inc(vec_const, 1)
            dve.wait_ge(vec_const, 8)
            w.tensor_scalar(snorm[:, 3, :], snorm[:, 3, :], 0.5 / SIM_SCALE, 1e-12 / SIM_SCALE, ALU.mult,
                            ALU.max).then_inc(vec_const, 1)
            dve.wait_ge(vec_const, 9)
            w.reciprocal(snorm[:, 3, :], snorm[:, 3, :]).then_inc(vec_const, 1)
            dve.wait_ge(vec_const, 10)
            w.tensor_tensor(simf[:], simf[:], snorm[:, 3, :].unsqueeze(1).broadcast_to([P, CH, NE]),
                            ALU.mult).then_inc(vec_const, 1)
            dve.wait_ge(act_const, 3)
            w.tensor_scalar(negA[:], negA[:], -1.0, None, ALU.mult).then_inc(vec_const, 1)
            w.tensor_scalar(sgate[:], sgate[:], 1.0, None, ALU.add).then_inc(vec_const, 1)
            dve.wait_ge(vec_const, 13)
            w.reciprocal(sgate[:], sgate[:]).then_inc(vec_const, 1)
            dve.wait_ge(act_const, 4)
            w.scalar_tensor_tensor(out=wlo[:], in0=wraw, scalar=wmax[:, 2:3], in1=whi[:], op0=ALU.mult,
                                   op1=ALU.subtract).then_inc(vec_const, 1)
            dve.wait_ge(act_const, 5)
            w.tensor_tensor(simlo[:], simf[:], simhi[:], ALU.subtract).then_inc(vec_const, 1)
            dve.wait_ge(vec_const, 16)
            dve.wait_ge(pool_const, 9)

            def statistics(s, steps, b, src, st, mv, sm):
                for t in range(T):
                    ins = w.bn_stats(st[:, t, :], src[:, t, :])
                ins.then_inc(s, 1)
                dve.wait_ge(s, step(steps, "stats", b))
                stand(dve)
                for t in range(T):
                    ins = w.bn_aggr(mv[:, t, :], st[:, t, :])
                ins.then_inc(s, 1)
                dve.wait_ge(s, step(steps, "aggr", b))
                w.tensor_scalar(sm[:, 0, :], mv[:, :, 1], EPS, None, ALU.add).then_inc(s, 1)

            def newton_rstd(s, steps, b, mv, sm):
                w.tensor_tensor(sm[:, 3, :], sm[:, 2, :], sm[:, 2, :], ALU.mult).then_inc(s, 1)
                dve.wait_ge(s, step(steps, "sq", b))
                w.tensor_tensor(sm[:, 3, :], sm[:, 3, :], sm[:, 0, :], ALU.mult).then_inc(s, 1)
                dve.wait_ge(s, step(steps, "vsq", b))
                w.tensor_scalar(sm[:, 3, :], sm[:, 3, :], -0.5, 1.5, ALU.mult, ALU.add).then_inc(s, 1)
                dve.wait_ge(s, step(steps, "cor", b))
                w.tensor_tensor(sm[:, 4, :], sm[:, 2, :], sm[:, 3, :], ALU.mult).then_inc(s, 1)
                dve.wait_ge(s, step(steps, "rstd", b))
                w.scalar_tensor_tensor(out=sm[:, 5, :], in0=mv[:, :, 0], scalar=-1.0, in1=sm[:, 4, :], op0=ALU.mult,
                                       op1=ALU.mult).then_inc(s, 1)

            def scan(i, n, half):
                dve.wait_ge(abar_done, i * 2 * NS + 2 * n + half + 1)
                if half == 0:
                    dve.wait_ge(v_done, i * NS + n + 1)
                    wait(dve, hT_full, i * 2 * NS + 2 * (n - 1))
                w.tensor_tensor_scan(h[:, n % 2, half, :], ab[half][:], v[:, n % 2, half, :], 0.0,
                                     ALU.mult, ALU.add).then_inc(scan_done, 1)

            def readout(i, n, k):
                dve.wait_ge(hT_full, i * 2 * NS + 2 * n + k + 1)
                if n == 0 and k == 0:
                    dve.wait_ge(pool_prep, step(POOL_PREP, "yinit", i))
                    dve.wait_ge(c_moved, (i + 1) * 16)
                if n == 0 and k == 1:
                    wait(dve, added_c, i * SCALES)
                if n > 0:
                    dve.wait_ge(read_out, read_by_vector(i, n - 1 - k, k))
                if n == NS - 1 and (not isinstance(i, int) or i > 0):
                    dve.wait_ge(pool_proj, i)
                    dve.wait_ge(x2b_moved, i * 16)
                src = y_next if n == 0 else y
                dst = x2a if n == NS - 1 else y
                for t in (2 * k, 2 * k + 1):
                    ins = w.scalar_tensor_tensor(out=dst[:, t, :], in0=hT[k][:, (t % 2) * D:(t % 2 + 1) * D],
                                                 scalar=ccur[:, t, n:n + 1], in1=src[:, t, :], op0=ALU.mult,
                                                 op1=ALU.add)
                ins.then_inc(read_out, 1)

            def combine(i, e):
                b = i - 1
                if e == 0:
                    dve.wait_ge(vec_gate, step(VEC_GATE, "rws", b))
                if e == NE - 1 and "attend" in stages_of(i):
                    dve.wait_ge(mb_full[0], bank_use(0, i, "pv"))
                for k in range(2):
                    dve.wait_ge(mb_full[2 + k], bank_use(2 + k, i, f"e{e}"))
                    if e > 0:
                        dve.wait_ge(mb_read[2 + k], bank_use(2 + k, i, f"e{e - 1}"))
                    for t in (2 * k, 2 * k + 1):
                        src = mb[2 + k][:, (t % 2) * QKV:(t % 2 + 1) * QKV]
                        if e == 0:
                            ins = w.tensor_scalar(acc[:, t, :], src, rws[:, t, e:e + 1], None, ALU.mult)
                        else:
                            dst = qkv if e == NE - 1 else acc
                            ins = w.scalar_tensor_tensor(out=dst[:, t, :], in0=src, scalar=rws[:, t, e:e + 1],
                                                         in1=acc[:, t, :], op0=ALU.mult, op1=ALU.add)
                    ins.then_inc(mb_read[2 + k], 1)

            def gating(i):
                b = i - 1
                k = vec_gate

                def at_step(name):
                    dve.wait_ge(k, step(VEC_GATE, name, b))

                dve.wait_ge(vec_proj, step(VEC_PROJ, "r", b))
                dve.wait_ge(mb_full[2], bank_use(2, i, "logit"))
                for t in range(T):
                    ins = w.scalar_tensor_tensor(out=lg[:, t, :], in0=mb[2][:, t * NE:(t + 1) * NE],
                                                 scalar=sm2[:, 13, t:t + 1], in1=sgate[:], op0=ALU.mult,
                                                 op1=ALU.subtract)
                ins.then_inc(mb_read[2], 1)
                dve.wait_ge(mb_read[2], bank_use(2, i, "logit"))
                stand(dve)
                for t in range(T):
                    ins = w.max(top8[:, t, :], lg[:, t, :])
                ins.then_inc(k, 1)
                at_step("top")
                first, second = top8[:, :, 0], top8[:, :, 1]
                w.tensor_tensor(g1[:, 0], lg[:], over_experts(second), ALU.is_gt).then_inc(k, 1)
                w.tensor_tensor(g1[:, 1], lg[:], over_experts(second), ALU.is_equal).then_inc(k, 1)
                at_step("eq")
                w.tensor_tensor_scan(g1[:, 2].rearrange("p t e -> p (t e)"), restart[:].rearrange("p t e -> p (t e)"),
                                     g1[:, 1].rearrange("p t e -> p (t e)"), 0.0, ALU.mult, ALU.add).then_inc(k, 1)
                w.tensor_tensor(gs[:, 0, :], first, second, ALU.is_le).then_inc(k, 1)
                at_step("room")
                w.scalar_tensor_tensor(out=g1[:, 3], in0=g1[:, 2], scalar=-1.0, in1=over_experts(gs[:, 0, :]),
                                       op0=ALU.add, op1=ALU.is_le).then_inc(k, 1)
                at_step("fit")
                w.tensor_tensor(g1[:, 4], g1[:, 3], g1[:, 1], ALU.mult).then_inc(k, 1)
                at_step("take")
                w.tensor_tensor(g1[:, 4], g1[:, 4], g1[:, 0], ALU.add).then_inc(k, 1)
                w.tensor_scalar(gs[:, 1, :], first, 0.0, None, ALU.is_le).then_inc(k, 1)
                at_step("idle")
                w.tensor_tensor(g1[:, 5], g1[:, 4], over_experts(gs[:, 1, :]), ALU.mult).then_inc(k, 1)
                at_step("fbm")
                w.scalar_tensor_tensor(out=g1[:, 6], in0=lg[:], scalar=0.0, in1=g1[:, 5], op0=ALU.is_gt,
                                       op1=ALU.max).then_inc(k, 1)
                w.tensor_scalar(g1[:, 7], lg[:], 0.0, None, ALU.max).then_inc(k, 1)
                w.tensor_scalar(gs[:, 2, :], first, 0.0, None, ALU.max).then_inc(k, 1)
                at_step("gmax")
                w.tensor_tensor(g1[:, 8], g1[:, 7], over_experts(gs[:, 2, :]), ALU.subtract).then_inc(k, 1)
                dve.wait_ge(act_gate, b + 1)
                w.tensor_tensor(g1[:, 9], ex[:], g1[:, 6], ALU.mult).then_inc(k, 1)
                at_step("kept")
                w.tensor_reduce(gs[:, 3, :], g1[:, 9], AX_X, ALU.add).then_inc(k, 1)
                at_step("sum")
                w.reciprocal(gs[:, 4, :], gs[:, 3, :]).then_inc(k, 1)
                at_step("rsum")
                w.tensor_tensor(rw[:], g1[:, 9], over_experts(gs[:, 4, :]), ALU.mult).then_inc(k, 1)
                at_step("rw")
                w.tensor_scalar(rws[:], rw[:], wmax[:, 3:4], None, ALU.mult).then_inc(k, 1)

            def one(i):
                on = stages_of(i)
                for n in range(NS):
                    if "scan" in on:
                        scan(i, n, 0)
                        if n > 0:
                            readout(i, n - 1, 0)
                        scan(i, n, 1)
                        if n > 0 and n % 2 == 1:
                            readout(i, n - 1, 1)
                    experts = EXPERTS_AT.get(n, []) if "project" in on else []
                    if "output" in on and n in OUT_AT:
                        t = OUT_AT[n]
                        k = 2 + t % 2
                        if t == 0:
                            wait(dve, out_stored, (i - 3) * 16)
                            dve.wait_ge(x2c_moved, (i - 2) * 16)
                        dve.wait_ge(mb_full[k], bank_use(k, i, f"op{t}"))
                        w.tensor_tensor(outt[:, t, :], mb[k][:, 0:D], x2c[:, t, :], ALU.add).then_inc(mb_read[k], 1)
                    for e in experts[:1]:
                        combine(i, e)
                    if "attend" in on:
                        b = i - 2
                        if n == 0:
                            w.tensor_copy(rwb[:], rw[:]).then_inc(vec_att, 1)
                        if n in (6, 8):
                            for t in (n - 6, n - 5):
                                dve.wait_ge(mb_full[t % 2], bank_use(t % 2, i, f"s{t}"))
                                w.tensor_reduce(mx[:, t:t + 1], mb[t % 2][:, 0:(t + 1) * P], AX_X,
                                                ALU.max).then_inc(vec_att, 1)
                                dve.wait_ge(vec_att, step(VEC_ATT, f"mx{t}", b))
                                w.tensor_scalar(nb[:, t:t + 1], mx[:, t:t + 1], -(HD ** -0.5), None,
                                                ALU.mult).then_inc(vec_att, 1)
                        if n == 9:
                            dve.wait_ge(mb_read[0], bank_use(0, i, "s2"))
                            dve.wait_ge(mb_read[1], bank_use(1, i, "s3"))
                            w.reciprocal(rinv[:], rs[:]).then_inc(vec_att, 1)
                            dve.wait_ge(vec_att, step(VEC_ATT, "rinv", b))
                            wait(dve, mixed, b * T)
                            w.tensor_tensor(rwn[:], rwb[:], over_experts(rinv[:]), ALU.mult).then_inc(vec_att, 1)
                    if "project" in on:
                        b = i - 1
                        if n == 0:
                            dve.wait_ge(read_out, i * READS)
                            dve.wait_ge(added_c, i * SCALES)
                            statistics(vec_proj, VEC_PROJ, b, x2a, st2, mv2, sm2)
                        if n == 1:
                            dve.wait_ge(act_proj, step(ACT_PROJ, "y0", b))
                            newton_rstd(vec_proj, VEC_PROJ, b, mv2, sm2)
                            w.tensor_tensor(sm2[:, 6, :], sm2[:, 4, :], sm2[:, 4, :], ALU.mult).then_inc(vec_proj, 1)
                            dve.wait_ge(vec_proj, step(VEC_PROJ, "rr", b))
                            w.scalar_tensor_tensor(out=sm2[:, 6, :], in0=sm2[:, 6, :], scalar=float(D),
                                                   in1=mv2[:, :, 1], op0=ALU.mult, op1=ALU.mult).then_inc(vec_proj, 1)
                            dve.wait_ge(vec_proj, step(VEC_PROJ, "ss", b))
                            w.tensor_scalar(sm2[:, 7, :], sm2[:, 6, :], NORM_MIN_SQ, None,
                                            ALU.max).then_inc(vec_proj, 1)
                            dve.wait_ge(act_proj, step(ACT_PROJ, "y2", b))
                            w.tensor_scalar(sm2[:, 10, :], sm2[:, 9, :], 2.0 ** 20, None,
                                            ALU.mult).then_inc(vec_proj, 1)
                            dve.wait_ge(vec_proj, step(VEC_PROJ, "y", b))
                            w.tensor_tensor(sm2[:, 11, :], sm2[:, 10, :], sm2[:, 10, :], ALU.mult).then_inc(vec_proj, 1)
                            dve.wait_ge(vec_proj, step(VEC_PROJ, "ysq", b))
                            w.tensor_tensor(sm2[:, 11, :], sm2[:, 11, :], sm2[:, 7, :], ALU.mult).then_inc(vec_proj, 1)
                            dve.wait_ge(vec_proj, step(VEC_PROJ, "yv", b))
                            w.tensor_scalar(sm2[:, 12, :], sm2[:, 11, :], -0.5, 1.5, ALU.mult,
                                            ALU.add).then_inc(vec_proj, 1)
                            dve.wait_ge(vec_proj, step(VEC_PROJ, "ycor", b))
                            w.scalar_tensor_tensor(out=sm2[:, 13, :], in0=sm2[:, 10, :], scalar=1.0 / SIM_SCALE,
                                                   in1=sm2[:, 12, :], op0=ALU.mult, op1=ALU.mult).then_inc(vec_proj, 1)
                        if n == 2:
                            for k in range(CH):
                                dve.wait_ge(act_proj, step(ACT_PROJ, f"hi{k}", b))
                                w.tensor_tensor(xlo[:, k, :], mb[k][:], xhi[:, k, :],
                                                ALU.subtract).then_inc(mb_read[k], 1)
                        if n == 3:
                            gating(i)
                    if "prepare" in on:
                        b = i + 1
                        if n == 4:
                            dve.wait_ge(x_loaded, (b + 1) * 16)
                            statistics(vec_prep, VEC_PREP, b, xt, st1, mv1, sm1)
                        if n == 5:
                            dve.wait_ge(act_prep, step(ACT_PREP, "y0", b))
                            newton_rstd(vec_prep, VEC_PREP, b, mv1, sm1)
                        if n == 11:
                            dve.wait_ge(act_prep, step(ACT_PREP, "softplus", b))
                            wait(dve, dt_moved, b * 16)
                            wait(dve, pool_prep, step(POOL_PREP, "u", i))
                            for k in range(CH):
                                w.scalar_tensor_tensor(out=dt_next[:, k, :], in0=mb[k][:], scalar=0.0,
                                                       in1=sp[:, k, :], op0=ALU.max,
                                                       op1=ALU.add).then_inc(mb_read[k], 1)
                    for e in experts[1:]:
                        combine(i, e)
                if "scan" in on:
                    readout(i, NS - 1, 0)

            iterations(dve, one)

        @block.tensor
        def _(pe):
            m = nc.tensor
            pe.wait_ge(const_loaded, NCONST * 16)
            pe.wait_ge(pool_const, 9)
            pe.wait_ge(vec_const, 2)
            for k in range(CH):
                ins = m.matmul(mb[0][:, 0:NE], ones[:], simsq[:, k, :], start=k == 0, stop=k == CH - 1)
            ins.then_inc(pe_const, 1)
            pe.wait_ge(vec_const, 16)

            def claim(k, i, what):
                wait(pe, mb_read[k], bank_use(k, i, what) - 1)

            def turn_h(i, n):
                pe.wait_ge(scan_done, i * 2 * NS + 2 * n + 2)
                for k in range(2):
                    if k == 1 and n % 2 == 0:
                        wait(pe, scaled_c, i * SCALES + n // 2)
                    else:
                        wait(pe, read_out, read_by_vector(i, n - 1, k))
                    for t in (2 * k, 2 * k + 1):
                        for half in range(CH):
                            c = (t % 2) * D + half * P
                            ins = m.transpose(hT[k][:, c:c + P], h[:, n % 2, half, t * P:(t + 1) * P], ident[:])
                    ins.then_inc(hT_full, 1)

            def project(i, e):
                for k in range(2):
                    claim(2 + k, i, f"e{e}")
                    for t in (2 * k, 2 * k + 1):
                        dst = mb[2 + k][:, (t % 2) * QKV:(t % 2 + 1) * QKV]
                        parts = [(s, wt, c) for c in range(CH) for s, wt in ((xhi, whi), (xhi, wlo), (xlo, whi))]
                        for j, (s, wt, c) in enumerate(parts):
                            ins = m.matmul(dst, s[:, c, t * P:(t + 1) * P], wt[:, c, e * QKV:(e + 1) * QKV],
                                           start=j == 0, stop=j == len(parts) - 1)
                    ins.then_inc(mb_full[2 + k], 1)

            def scores(i, t):
                k = t % 2
                claim(k, i, f"s{t}")
                w = (t + 1) * P
                m.matmul(mb[k][:, 0:w], qT[:, t * P:(t + 1) * P], kT[:, 0:w], start=True, stop=False)
                m.matmul(mb[k][:, t * P:w], identb[:], causal[:], start=False, stop=True).then_inc(mb_full[k], 1)

            def turn_mix(i, t):
                pe.wait_ge(mixed, (i - 3) * T + t + 1)
                for k in range(2):
                    claim(k, i, f"mix{t}")
                    for c in range(4):
                        e = 2 * (4 * k + c)
                        ins = m.transpose(mb[k][:, c * P:(c + 1) * P],
                                          mix[:, t % 2, e:e + 2, :].rearrange("p e d -> p (e d)"), ident[:])
                    ins.then_inc(mb_full[k], 1)

            def out_projection(i, t):
                k = 2 + t % 2
                claim(k, i, f"op{t}")
                pe.wait_ge(mb_read[0], bank_use(0, i, f"mix{t}"))
                pe.wait_ge(mb_read[1], bank_use(1, i, f"mix{t}"))
                for j in range(KO):
                    ins = m.matmul(mb[k][:, 0:D], mixT[:, j, :], wo[:, j, :], start=j == 0, stop=j == KO - 1)
                ins.then_inc(mb_full[k], 1)

            def turn(i, k, what, src):
                claim(k, i, what)
                stand(pe)
                for c, block_ in enumerate(src):
                    ins = m.transpose(mb[k][0:block_.shape[1], c * P:(c + 1) * P], block_, ident[:])
                ins.then_inc(mb_full[k], 1)

            def one(i):
                on = stages_of(i)
                for n in range(NS):
                    if "scan" in on and n > 0:
                        turn_h(i, n - 1)
                    experts = EXPERTS_AT.get(n, []) if "project" in on else []
                    if "output" in on:
                        if n in OUT_AT:
                            out_projection(i, OUT_AT[n])
                        if n in TURN_AT:
                            turn_mix(i, TURN_AT[n])
                    for e in experts[:1]:
                        project(i, e)
                    if "project" in on:
                        if n == 2:
                            pe.wait_ge(pool_proj, i)
                            for k in range(CH):
                                turn(i, k, "xh", [xh[:, t, k * P:(k + 1) * P] for t in range(T)])
                        if n == 3:
                            claim(2, i, "logit")
                            pe.wait_ge(mb_read[0], bank_use(0, i, "xh"))
                            pe.wait_ge(mb_read[1], bank_use(1, i, "xh"))
                            for t in range(T):
                                parts = [(s, wt, c) for c in range(CH)
                                         for s, wt in ((xhi, simhi), (xhi, simlo), (xlo, simhi))]
                                for j, (s, wt, c) in enumerate(parts):
                                    ins = m.matmul(mb[2][:, t * NE:(t + 1) * NE], s[:, c, t * P:(t + 1) * P],
                                                   wt[:, c, :], start=j == 0, stop=j == len(parts) - 1)
                            ins.then_inc(mb_full[2], 1)
                    if "attend" in on:
                        if n == 5:
                            if "project" in on:
                                pe.wait_ge(mb_read[2], bank_use(2, i - 1, f"e{NE - 1}"))
                                pe.wait_ge(mb_read[3], bank_use(3, i - 1, f"e{NE - 1}"))
                            else:
                                pe.wait_ge(mb_read[2], bank_use(2, NB, f"e{NE - 1}"))
                                pe.wait_ge(mb_read[3], bank_use(3, NB, f"e{NE - 1}"))
                            for k in range(2):
                                turn(i, k, "qk"[k], [qkv[:, t, k * HD:(k + 1) * HD] for t in range(T)])
                        if n in (6, 8):
                            if n == 6:
                                pe.wait_ge(mb_read[0], bank_use(0, i, "q"))
                                pe.wait_ge(mb_read[1], bank_use(1, i, "k"))
                            scores(i, n - 6)
                            scores(i, n - 5)
                        if n == 10:
                            pe.wait_ge(mb_read[0], bank_use(0, i, "s2"))
                            pe.wait_ge(mb_read[1], bank_use(1, i, "s3"))
                            turn(i, 0, "pt1", [pr[:, t, P:2 * P] for t in range(1, T)])
                            turn(i, 1, "pt0", [pr[:, t, 0:P] for t in range(T)])
                        if n == 12:
                            turn(i, 0, "pt23", [pr[:, 2, 2 * P:3 * P], pr[:, 3, 2 * P:3 * P], pr[:, 3, 2 * P:3 * P],
                                                pr[:, 3, 3 * P:4 * P]])
                        if n == 13:
                            claim(0, i, "pv")
                            pe.wait_ge(mb_read[1], bank_use(1, i, "pt0"))
                            for t in range(T):
                                for j in range(t + 1):
                                    ins = m.matmul(mb[0][:, t * HD:(t + 1) * HD], pt[:, j, t * P:(t + 1) * P],
                                                   qkv[:, j, 2 * HD:3 * HD], start=j == 0, stop=j == t)
                            ins.then_inc(mb_full[0], 1)
                    if "prepare" in on:
                        if n == 7:
                            pe.wait_ge(pool_prep, step(POOL_PREP, "xn", i + 1))
                            for k in range(CH):
                                turn(i, k, "xn", [xn[:, t, k * P:(k + 1) * P] for t in range(T)])
                        if n == 9:
                            claim(0, i, "dtl")
                            pe.wait_ge(mb_read[1], bank_use(1, i, "xn"))
                            for k in range(CH):
                                ins = m.matmul(mb[0][0:RANK + NS, :], wx[:, k, 0:RANK + NS], xnT[:, k, :],
                                               start=k == 0, stop=k == CH - 1)
                            ins.then_inc(mb_full[0], 1)
                            claim(1, i, "c")
                            for t in range(T):
                                for k in range(CH):
                                    ins = m.matmul(mb[1][:, t * NS:(t + 1) * NS], xnT[:, k, t * P:(t + 1) * P],
                                                   wx[:, k, RANK + NS:], start=k == 0, stop=k == CH - 1)
                            ins.then_inc(mb_full[1], 1)
                        if n == 11:
                            pe.wait_ge(mb_read[0], bank_use(0, i, "dtl"))
                            for k in range(CH):
                                claim(k, i, "dtp")
                                m.matmul(mb[k][:], wdt[:, k * P:(k + 1) * P], dtl[:], start=True,
                                         stop=True).then_inc(mb_full[k], 1)
                    for e in experts[1:]:
                        project(i, e)
                if "scan" in on:
                    turn_h(i, NS - 1)

            iterations(pe, one)


_OUT = (NB, L, D)


def kernel(**inputs):
    import numpy as np
    import concourse.bacc as bacc
    from concourse.bass_utils import run_bass_kernel_spmd

    def take(name):
        return np.asarray(inputs[name])

    arrays = {
        "x": take("L0_attn_x"),
        "A_log": take("L0_attn_A_log"),
        "D_param": take("L0_attn_D_param").reshape(1, D),
        "WxT": take("L0_attn_W_x").T,
        "WdtT": take("L0_attn_W_dt").T,
        "b_dt": take("L0_attn_b_dt").reshape(1, D),
        "sim": take("L0_ffn_sim_matrix"),
        "gates": take("L0_ffn_gates").reshape(1, NE),
        "Wqkv": np.stack([take(f"L0_ffn_{n}_proj") for n in "qkv"], 2).transpose(1, 0, 2, 3).reshape(D, NE * QKV),
        "Wo": take("L0_ffn_o_proj").reshape(NE * HD, D),
    }
    arrays = {k: np.ascontiguousarray(a) for k, a in arrays.items()}
    nc = bacc.Bacc("TRN2", target_bir_lowering=False, num_devices=1)
    args = [nc.dram_tensor(f"{k}_dram", a.shape, mybir.dt.from_np(a.dtype), kind="ExternalInput").ap()
            for k, a in arrays.items()]
    args.append(nc.dram_tensor("b_rows", (NS, L), F32, kind="Internal").ap())
    args.append(nc.dram_tensor("out_dram", _OUT, F32, kind="ExternalOutput").ap())
    scan_attention_kernel(nc, *args)
    r = run_bass_kernel_spmd(nc, [{f"{k}_dram": a for k, a in arrays.items()}], core_ids=[0])
    return r.results[0]["out_dram"]
```

```python
from contextlib import ExitStack

import concourse.bass as bass
from concourse import mybir

ALU = mybir.AluOpType
ACT = mybir.ActivationFunctionType
F32 = mybir.dt.float32
F16 = mybir.dt.float16
BF16 = mybir.dt.bfloat16
AX_X = mybir.AxisListType.X

P = 128
NB, L, D = 16, 512, 256
NS, RANK = 16, 64
NE, HD = 16, 64
T = L // P
CH = D // P
QKV = 3 * HD
KO = NE * HD // P
EPS = 1e-5
NORM_MIN_SQ = 1e-24
SIM_SCALE = 64.0
W_TOP = 256.0
MASKED = -1e30
BG = 4

EXPERTS_AT = {7: [0, 1], 8: [2], 9: [3], 10: [4], 11: [5, 6], 12: [7], 13: [8, 9], 14: [10, 11], 15: [12, 13]}
LATE_AT = {0: [14], 3: [15]}
LATE = [e for es in LATE_AT.values() for e in es]
FIRST_EXPERT = min(EXPERTS_AT)
TURN_AT = {0: 0, 1: 1, 3: 2, 5: 3}
OUT_AT = {1: 0, 2: 1, 4: 2, 6: 3}
RESIDUAL_AT = {2: 0, 3: 1, 5: 2, 6: 3}


def bank_uses():
    uses = []
    for n in range(NS):
        late, experts = LATE_AT.get(n, []), EXPERTS_AT.get(n, [])
        for e in late:
            uses += [(f"e{e}.{k}", "attend") for k in range(2)]
        uses += {3: [("xh.0", "project"), ("xh.1", "project")], 5: [("logit", "project")]}.get(n, [])
        uses += {5: [("q", "attend"), ("k", "attend")], 6: [("s0", "attend"), ("s1", "attend")],
                 8: [("s2", "attend"), ("s3", "attend")], 11: [("pt1", "attend"), ("pt0", "attend")],
                 12: [("pt23", "attend")], 13: [("pv", "attend")]}.get(n, [])
        if n in OUT_AT:
            uses += [(f"op{OUT_AT[n]}", "output")]
        if n in TURN_AT:
            uses += [(f"mix{TURN_AT[n]}.{k}", "output") for k in range(2)]
        for e in experts[:1]:
            uses += [(f"e{e}.{k}", "project") for k in range(2)]
        uses += {7: [("xn.0", "prepare"), ("xn.1", "prepare")], 9: [("dtl", "prepare"), ("c", "prepare")],
                 10: [("dtp.0", "prepare"), ("dtp.1", "prepare")]}.get(n, [])
        for e in experts[1:]:
            uses += [(f"e{e}.{k}", "project") for k in range(2)]
    return uses


BANKS = 4
ALL_USES = bank_uses()
BANK_USES = [ALL_USES[k::BANKS] for k in range(BANKS)]
BANK_OF = {what: j % BANKS for j, (what, _) in enumerate(ALL_USES)}
STAGE_OF = dict(ALL_USES)


def stages_of(i):
    if not isinstance(i, int):
        return {"prepare", "scan", "project", "attend", "output"}
    lag = {"prepare": -1, "scan": 0, "project": 1, "attend": 2, "output": 3}
    return {stage for stage, d in lag.items() if 0 <= i - d < NB}


def bank_use(i, what):
    uses = BANK_USES[BANK_OF[what]]
    lag = {"prepare": -1, "project": 1, "attend": 2, "output": 3}
    per = {s: sum(1 for _, stage in uses if stage == s) for s in lag}
    on = stages_of(i)
    inside = 0
    for name, stage in uses:
        if stage in on:
            inside += 1
        if name == what:
            break
    if isinstance(i, int):
        return inside + sum(per[s] * min(max(i - lag[s], 0), NB) for s in lag)
    return i * len(uses) + (inside - sum(per[s] * lag[s] for s in lag))


VEC_SETUP = ["simsq", "floor", "inv", "quot", "sum", "norm", "invnorm", "sim", "negA", "sg1", "sgate", "simlo"]
ACT_SETUP = ["sqrt", "expA", "expg", "simhi"]
VEC_SPLIT = ["max0", "max1", "max", "unscale", "scale", "lo0", "lo1", "lo2", "lo3"]
ACT_SPLIT = ["hi0", "hi1", "hi2", "hi3"]
VEC_PREP = ["stats", "aggr", "var", "sq", "vsq", "cor", "rstd", "nmr", "dt"]
ACT_PREP = ["ln", "y0", "xn", "abs", "exp", "softplus"]
POOL_PREP = ["skip", "yinit", "u"]
VEC_PROJ = ["stats", "aggr", "var", "sq", "vsq", "cor", "rstd", "nmr", "rr", "ss", "ssc", "y", "ysq", "yv",
            "ycor", "r"]
ACT_PROJ = ["ln", "y0", "xh", "ln2", "y2", "hi0", "hi1"]
VEC_GATE = ["top", "strict", "eq", "rank", "room", "fit", "take", "fb", "idle", "fbm", "mask", "gated", "gmax",
            "shift", "kept", "sum", "rsum", "rw", "rws"]
VEC_ATT = ["rwb", "mx0", "nb0", "mx1", "nb1", "mx2", "nb2", "mx3", "nb3", "rinv", "rwn"]


READS = NS + NS // 2
SCALES = NS // 2


def read_by_vector(b, n, k):
    return b * READS + (n // 2 * 3 + (3 if n % 2 else k + 1))


def step(steps, name, b):
    return b * len(steps) + (steps.index(name) + 1)


def scan_attention_kernel(nc, x, A_log, D_param, WxT, WdtT, b_dt, sim, gates, Wqkv, Wo, b_rows, out):
    with ExitStack() as ctx:
        def sb(name, shape, dt=F32):
            return ctx.enter_context(nc.sbuf_tensor(name, shape, dt))

        def bank(name):
            return ctx.enter_context(nc.psum_tensor(name, [P, 512], F32))

        def sem(name):
            return ctx.enter_context(nc.semaphore(name))

        ident = sb("ident", [P, P])
        identb = sb("identb", [P, P], BF16)
        causal = sb("causal", [P, P], BF16)
        ones = sb("ones", [P, P])
        restart = sb("restart", [P, T, NE])
        wx = sb("wx", [P, CH, RANK + 2 * NS])
        wdt = sb("wdt", [RANK + NS + 1, D])
        negA = sb("negA", [P, CH, NS])
        dskip = sb("dskip", [P, D])
        sgate = sb("sgate", [P, NE])
        simf = sb("simf", [P, CH, NE])
        simsq = sb("simsq", [P, CH, NE])
        simhi = sb("simhi", [P, CH, NE], F16)
        simlo = sb("simlo", [P, CH, NE], F16)
        snorm = sb("snorm", [P, 4, NE])
        wmax = sb("wmax", [P, 6])
        whi = sb("whi", [P, CH, NE * QKV], F16)
        wlo = sb("wlo", [P, CH, NE * QKV], F16)
        wo = sb("wo", [P, KO, D])
        xt = sb("xt", [P, T, D])
        xnT = sb("xnT", [P, CH, L])
        dtl = sb("dtl", [RANK + NS + 1, L])
        norm = sb("norm", [P, 2 * L])
        xh = norm[:].rearrange("p (t c) -> p t c", t=T)
        xn = norm[:].rearrange("p (t c) -> p t c", t=T)
        sp = norm[:].rearrange("p (h l) -> p h l", h=CH)
        dt_next = sb("dt_next", [P, CH, L])
        u_next = sb("u_next", [P, CH, L])
        y_next = sb("y_next", [P, T, D])
        c_next = sb("c_next", [P, T, NS])
        st1 = sb("st1", [P, T, 6])
        mv1 = sb("mv1", [P, T, 2])
        sm1 = sb("sm1", [P, 6, T])
        dt = sb("dt", [P, CH, L])
        u = sb("u", [P, CH, L])
        y = sb("y", [P, T, D])
        ccur = sb("ccur", [P, T, NS])
        bb = sb("bb", [P, NS, L])
        v = sb("v", [P, 4, CH, L])
        abar = sb("abar", [P, 2, CH, L])
        ytmp = sb("ytmp", [P, 2, 2, D])
        yodd = sb("yodd", [P, 2, D])
        h = sb("h", [P, 2, CH, L])
        x2a = sb("x2a", [P, T, D])
        xhi = sb("xhi", [P, CH, L], F16)
        xlo = sb("xlo", [P, CH, L], F16)
        st2 = sb("st2", [P, T, 6])
        mv2 = sb("mv2", [P, T, 2])
        sm2 = sb("sm2", [P, 14, T])
        lg = sb("lg", [P, T, NE])
        top8 = sb("top8", [P, T, 8])
        g1 = sb("g1", [P, 10, T, NE])
        gs = sb("gs", [P, 6, T])
        ex = sb("ex", [P, T, NE])
        rw = sb("rw", [P, T, NE])
        rws = sb("rws", [P, T, NE])
        acc = sb("acc", [P, T, QKV])
        qkv = sb("qkv", [P, T, QKV])
        late = sb("late", [P, 2 * T * L + 2 * T * D])
        pr = late[:, 0:T * L].rearrange("p (t l) -> p t l", t=T)
        pt = late[:, T * L:2 * T * L].rearrange("p (t l) -> p t l", t=T)
        x2b = late[:, 2 * T * L:2 * T * L + T * D].rearrange("p (t c) -> p t c", t=T)
        x2c = late[:, 2 * T * L + T * D:].rearrange("p (t c) -> p t c", t=T)
        mix = late[:, 0:2 * NE * HD].rearrange("p (k e d) -> p k e d", k=2, e=NE)
        wraw = late[:, 0:CH * NE * QKV].rearrange("p (h c) -> p h c", h=CH)
        rwb = sb("rwb", [P, T, NE])
        qT = sb("qT", [HD, L])
        kT = sb("kT", [HD, L])
        mx = sb("mx", [P, T])
        nb = sb("nb", [P, T])
        rs = sb("rs", [P, T])
        rinv = sb("rinv", [P, T])
        rwn = sb("rwn", [P, T, NE])
        at = sb("at", [P, T, HD])
        mixT = sb("mixT", [P, KO, P])
        outt = sb("outt", [P, T, D])

        hT = [[bank(f"hT{s}{k}") for k in range(2)] for s in range(2)]
        mb = [bank(f"mb{k}") for k in range(BANKS)]

        const_loaded = sem("const_loaded")
        pool_const = sem("pool_const")
        weights_loaded, wo_loaded = sem("weights_loaded"), sem("wo_loaded")
        pool_wmax = sem("pool_wmax")
        vec_setup, vec_wdt = sem("vec_setup"), sem("vec_wdt")
        act_setup = sem("act_setup")
        vec_split, act_split = sem("vec_split"), sem("act_split")
        pe_const = sem("pe_const")
        x_loaded = sem("x_loaded")
        dt_moved, u_moved, c_moved = sem("dt_moved"), sem("u_moved"), sem("c_moved")
        b_kept, b_spread = sem("b_kept"), [sem(f"b_spread{g}") for g in range(NS // BG)]
        x2b_moved, x2c_moved = sem("x2b_moved"), sem("x2c_moved")
        out_stored = sem("out_stored")
        vec_prep, act_prep, pool_prep = sem("vec_prep"), sem("act_prep"), sem("pool_prep")
        v_done = sem("v_done")
        abar_done = sem("abar_done")
        scan_done = sem("scan_done")
        hT_full = sem("hT_full")
        read_out = sem("read_out")
        scaled_c, added_c = sem("scaled_c"), sem("added_c")
        vec_proj, act_proj = sem("vec_proj"), sem("act_proj")
        vec_gate, act_gate = sem("vec_gate"), sem("act_gate")
        vec_att = sem("vec_att")
        mixed = sem("mixed")
        passed = sem("passed")
        mb_full = [sem(f"mb{k}_full") for k in range(BANKS)]
        mb_read = [sem(f"mb{k}_read") for k in range(BANKS)]

        def wait(eng, s, value):
            if not isinstance(value, int) or value > 0:
                eng.wait_ge(s, value)

        def stand(eng, i=None):
            eng.sem_inc(passed, 1)

        def shared(what):
            return mb[BANK_OF[what]]

        def filled(what):
            return mb_full[BANK_OF[what]]

        def freed(what):
            return mb_read[BANK_OF[what]]

        def wait_filled(eng, i, what):
            eng.wait_ge(filled(what), bank_use(i, what))

        def wait_read(eng, i, what):
            if STAGE_OF[what] in stages_of(i):
                eng.wait_ge(freed(what), bank_use(i, what))

        def late_from(i, e):
            return i if e in LATE else i - 1

        def iterations(eng, one):
            for i in range(-1, 4):
                one(i)
            with eng.Fori(4, NB - 1) as i:
                one(i)
            for i in range(NB - 1, NB + 3):
                one(i)

        def weight_part(j):
            half = NE * QKV // 2
            return j // 2, slice(j % 2 * half, (j % 2 + 1) * half)

        def over_tiles(ap):
            return ap.unsqueeze(1).broadcast_to([P, T, ap.shape[1]])

        def over_experts(ap):
            return ap.unsqueeze(2).broadcast_to([P, T, NE])

        NCONST = 7
        block = ctx.enter_context(nc.Block())

        @block.sync
        def _(sp_eng):
            e = sp_eng

            def load_x(b):
                e.dma_start(xt[:], x[b].rearrange("(t p) c -> p t c", p=P)).then_inc(x_loaded, 16)

            load_x(0)
            e.dma_start(wx[:], WxT.rearrange("(h p) k -> p h k", p=P)).then_inc(const_loaded, 16)
            e.wait_ge(vec_wdt, 1)
            e.dma_start(wdt[0:RANK, :], WdtT).then_inc(const_loaded, 16)
            e.dma_start(wdt[RANK + NS:RANK + NS + 1, :], b_dt).then_inc(const_loaded, 16)
            e.dma_start(negA[:], A_log.rearrange("(h p) n -> p h n", p=P)).then_inc(const_loaded, 16)
            e.dma_start(dskip[:], D_param.broadcast_to([P, D])).then_inc(const_loaded, 16)
            e.dma_start(sgate[:], gates.broadcast_to([P, NE])).then_inc(const_loaded, 16)
            e.dma_start(simf[:], sim.rearrange("(h p) n -> p h n", p=P)).then_inc(const_loaded, 16)
            e.dma_start(wraw, Wqkv.rearrange("(h p) n -> p h n", p=P)).then_inc(weights_loaded, 16)
            e.dma_start(wo[:], Wo.rearrange("(k p) c -> p k c", p=P)).then_inc(wo_loaded, 16)

            def one(i):
                on = stages_of(i)
                if "scan" in on:
                    wait(e, vec_prep, step(VEC_PREP, "dt", i))
                    stand(e)
                    wait(e, abar_done, i * 2 * NS)
                    e.dma_start(dt[:], dt_next[:]).then_inc(dt_moved, 16)
                    wait(e, pool_prep, step(POOL_PREP, "u", i))
                    stand(e)
                    wait(e, v_done, i * NS)
                    e.dma_start(u[:], u_next[:]).then_inc(u_moved, 16)
                if "prepare" in on and (not isinstance(i, int) or i >= 0):
                    wait(e, pool_prep, step(POOL_PREP, "yinit", i))
                    stand(e)
                    load_x(i + 1)
                if "scan" in on:
                    wait_read(e, i - 1, "c")
                    stand(e)
                    wait(e, read_out, i * READS)
                    stand(e)
                    wait(e, scaled_c, i * SCALES)
                    e.dma_start(ccur[:], c_next[:]).then_inc(c_moved, 16)
                if "output" in on:
                    wait_read(e, i, "op3")
                    stand(e)
                    e.dma_start(out[i - 3].rearrange("(t p) c -> p t c", p=P), outt[:]).then_inc(out_stored, 16)
                if "attend" in on:
                    wait(e, x2b_moved, (i - 1) * 16)
                    e.dma_start(x2c[:], x2b[:]).then_inc(x2c_moved, 16)
                if "project" in on:
                    wait(e, read_out, i * READS)
                    stand(e)
                    wait(e, added_c, i * SCALES)
                    stand(e)
                    wait(e, x2c_moved, (i - 1) * 16)
                    if isinstance(i, int) and i == 1:
                        e.wait_ge(vec_split, len(VEC_SPLIT))
                    e.dma_start(x2b[:], x2a[:]).then_inc(x2b_moved, 16)
                if "prepare" in on:
                    wait_read(e, i, "dtl")
                    stand(e)
                    for g in range(NS // BG):
                        wait(e, b_spread[g], (i + 1) * 16)
                        stand(e)
                    e.dma_start(b_rows, dtl[RANK:RANK + NS, :]).then_inc(b_kept, 16)
                    wait(e, b_kept, (i + 2) * 16)
                    for g in range(NS // BG):
                        if "scan" in on:
                            stand(e)
                            wait(e, v_done, i * NS + BG * (g + 1))
                        e.dma_start(bb[:, g * BG:(g + 1) * BG, :],
                                    b_rows[g * BG:(g + 1) * BG, :].partition_broadcast(P)).then_inc(b_spread[g], 16)

            iterations(e, one)
            e.wait_ge(out_stored, NB * 16)

        @block.gpsimd
        def _(pool):
            g = nc.gpsimd
            g.memset(ident[:], 0.0).then_inc(pool_const, 1)
            g.memset(causal[:], 0.0).then_inc(pool_const, 1)
            g.memset(ones[:], 1.0).then_inc(pool_const, 1)
            g.memset(dtl[:], 1.0).then_inc(pool_const, 1)
            g.memset(restart[:], 1.0).then_inc(pool_const, 1)
            pool.wait_ge(pool_const, 5)
            g.affine_select(out=ident[:], in_=ident[:], compare_op=ALU.not_equal, fill=1.0, base=0,
                            pattern=[[-1, P]], channel_multiplier=1).then_inc(pool_const, 1)
            g.affine_select(out=causal[:], in_=causal[:], compare_op=ALU.is_ge, fill=MASKED, base=0,
                            pattern=[[-1, P]], channel_multiplier=1).then_inc(pool_const, 1)
            g.memset(restart[:, :, 0:1], 0.0).then_inc(pool_const, 1)
            pool.wait_ge(pool_const, 6)
            g.tensor_copy(identb[:], ident[:]).then_inc(pool_const, 1)
            pool.wait_ge(const_loaded, NCONST * 16)

            def b_times_u(i, n, src):
                if n % BG == 0:
                    pool.wait_ge(b_spread[n // BG], (i + 1) * 16)
                wait(pool, scan_done, i * 2 * NS + 2 * (n - 3))
                g.tensor_tensor(v[:, n % 4], src[:], bb[:, n, :].unsqueeze(1).broadcast_to([P, CH, L]),
                                ALU.mult).then_inc(v_done, 1)

            def add_c(i, n):
                wait(pool, scaled_c, i * SCALES + n // 2 + 1)
                if n > 3:
                    stand(pool)
                    wait(pool, added_c, i * SCALES + n // 2 - 1)
                g.tensor_tensor(yodd[:], yodd[:], ytmp[:, n // 2 % 2], ALU.add).then_inc(added_c, 1)

            def join_sums(i):
                wait(pool, added_c, i * SCALES + SCALES - 1)
                stand(pool)
                wait(pool, read_out, read_by_vector(i, NS - 2, 1))
                if not isinstance(i, int) or i > 0:
                    stand(pool)
                    pool.wait_ge(act_proj, step(ACT_PROJ, "xh", i - 1))
                    stand(pool)
                    pool.wait_ge(x2b_moved, i * 16)
                g.tensor_tensor(x2a[:, 2:4, :], yodd[:], y[:, 2:4, :], ALU.add).then_inc(added_c, 1)

            def mix_heads(i, b, t):
                if t >= 2:
                    wait_filled(pool, i, f"mix{t - 2}.1")
                elif not isinstance(i, int) or i > 2:
                    wait_filled(pool, i, f"mix{t + 2}.1")
                g.tensor_tensor(mix[:, t % 2], at[:, t, :].unsqueeze(1).broadcast_to([P, NE, HD]),
                                rwn[:, t, :].unsqueeze(2).broadcast_to([P, NE, HD]),
                                ALU.mult).then_inc(mixed, 1)

            def one(i):
                on, before = stages_of(i), stages_of(i - 1)
                for n in range(NS):
                    if "scan" in before and n == 1:
                        add_c(i - 1, NS - 1)
                        join_sums(i - 1)
                    if "scan" in on:
                        if n == 0:
                            wait(pool, u_moved, (i + 1) * 16)
                        if n + 2 < NS:
                            b_times_u(i, n + 2, u)
                        if n >= 5 and n % 2 == 1:
                            add_c(i, n - 2)
                    if "output" in on and n in (1, 2):
                        mix_heads(i, i - 3, n + 1)
                    if isinstance(i, int) and i == 0 and n == 4:
                        pool.wait_ge(vec_split, step(VEC_SPLIT, "max", 0))
                        g.partition_all_reduce(wmax[:, 3:4], wmax[:, 2:3], P,
                                               bass.bass_isa.ReduceOp.max).then_inc(pool_wmax, 1)
                    if "prepare" in on:
                        if n == 7:
                            wait(pool, act_prep, step(ACT_PREP, "xn", i + 1))
                            if "scan" in on:
                                stand(pool)
                                wait(pool, read_out, read_by_vector(i, 0, 1))
                            g.tensor_tensor(y_next[:], xn[:], over_tiles(dskip[:]), ALU.mult).then_inc(pool_prep, 1)
                        if n == 8:
                            wait(pool, pool_prep, step(POOL_PREP, "skip", i + 1))
                            g.tensor_tensor(y_next[:], y_next[:], xt[:], ALU.add).then_inc(pool_prep, 1)
                        if n == 13:
                            wait(pool, vec_prep, step(VEC_PREP, "dt", i + 1))
                            if "scan" in on:
                                stand(pool)
                                wait(pool, u_moved, (i + 1) * 16)
                            g.tensor_tensor(u_next[:], dt_next[:], xnT[:], ALU.mult).then_inc(pool_prep, 1)
                        if n == 14:
                            wait(pool, pool_prep, step(POOL_PREP, "u", i + 1))
                        if n >= 14:
                            b_times_u(i + 1, n - 14, u_next)
                    if "attend" in on and n in (14, 15):
                        if n == 14:
                            wait(pool, vec_att, step(VEC_ATT, "rwn", i - 2))
                            stand(pool)
                            wait_read(pool, i, "pv")
                        mix_heads(i, i - 2, n - 14)

            iterations(pool, one)

        @block.scalar
        def _(act):
            a = nc.scalar
            act.wait_ge(const_loaded, NCONST * 16)
            act.wait_ge(vec_setup, step(VEC_SETUP, "floor", 0))
            a.activation(snorm[:, 1, :], snorm[:, 0, :], ACT.Sqrt).then_inc(act_setup, 1)
            a.preload_act_table_set("natural_log_exp_and_others")
            a.activation(negA[:], negA[:], ACT.Exp).then_inc(act_setup, 1)
            a.activation(sgate[:], sgate[:], ACT.Exp, scale=-1.0).then_inc(act_setup, 1)
            act.wait_ge(vec_setup, step(VEC_SETUP, "sim", 0))
            a.activation(simhi[:], simf[:], ACT.Copy).then_inc(act_setup, 1)

            def decay(i, n, half, src):
                wait(act, scan_done, i * 2 * NS + 2 * (n - 2) + half + 1)
                a.activation(abar[:, n % 2, half, :], src[:, half, :], ACT.Exp,
                             scale=negA[:, half, n:n + 1]).then_inc(abar_done, 1)

            def scale_c(i, n):
                act.wait_ge(hT_full, i * 2 * NS + 2 * n + 2)
                if n == 3:
                    act.wait_ge(c_moved, (i + 1) * 16)
                if n == 1:
                    wait(act, added_c, i * SCALES)
                    dst = yodd
                else:
                    wait(act, added_c, i * SCALES + n // 2 - 2)
                    dst = ytmp[:, n // 2 % 2]
                for t in (2, 3):
                    ins = a.activation(dst[:, t - 2, :], hT[1][1][:, (t - 2) * D:(t - 1) * D], ACT.Copy,
                                       scale=(c_next if n == 1 else ccur)[:, t, n:n + 1])
                ins.then_inc(scaled_c, 1)

            def empty(i, what, dst, src):
                wait_filled(act, i, what)
                a.activation(dst, src, ACT.Copy).then_inc(freed(what), 1)

            def one(i):
                on, before = stages_of(i), stages_of(i - 1)
                for n in range(NS):
                    if "scan" in on:
                        if n == 0:
                            wait(act, dt_moved, (i + 1) * 16)
                        if n + 1 < NS:
                            decay(i, n + 1, 0, dt)
                        if n >= 3 and n % 2 == 1:
                            scale_c(i, n - 2)
                        if n + 1 < NS:
                            decay(i, n + 1, 1, dt)
                    if "scan" in before and n == 1:
                        scale_c(i - 1, NS - 1)
                    if isinstance(i, int) and i == 0 and n in (5, 7, 9, 11):
                        act.wait_ge(vec_split, step(VEC_SPLIT, "scale", 0))
                        c, cols = weight_part((n - 5) // 2)
                        a.activation(whi[:, c, cols], wraw[:, c, cols], ACT.Copy,
                                     scale=wmax[:, 5:6]).then_inc(act_split, 1)
                    if "prepare" in on and n == 15:
                        wait(act, vec_prep, step(VEC_PREP, "dt", i + 1))
                        decay(i + 1, 0, 0, dt_next)
                        decay(i + 1, 0, 1, dt_next)
                    if "project" in on and n == 3:
                        for k in range(CH):
                            wait_filled(act, i, f"xh.{k}")
                            a.activation(xhi[:, k, :], shared(f"xh.{k}")[:], ACT.Copy).then_inc(act_proj, 1)
                    if "attend" in on:
                        b = i - 2
                        if n == 5:
                            empty(i, "q", qT[:], shared("q")[0:HD, :])
                            empty(i, "k", kT[:], shared("k")[0:HD, :])
                        if n in (6, 8):
                            for t in (n - 6, n - 5):
                                act.wait_ge(vec_att, step(VEC_ATT, f"nb{t}", b))
                                w = (t + 1) * P
                                a.activation(pr[:, t, 0:w], shared(f"s{t}")[:, 0:w], ACT.Exp, bias=nb[:, t:t + 1],
                                             scale=HD ** -0.5, accum_out=rs[:, t:t + 1]).then_inc(freed(f"s{t}"), 1)
                        if n == 11:
                            empty(i, "pt1", pt[:, 1, P:L], shared("pt1")[:, 0:L - P])
                            empty(i, "pt0", pt[:, 0, :], shared("pt0")[:])
                        if n == 12:
                            empty(i, "pt23", pt[:, 2:4, 2 * P:L], shared("pt23")[:].rearrange("p (a c) -> p a c", a=2))
                        if n == 13:
                            wait(act, mixed, b * T)
                            empty(i, "pv", at[:], shared("pv")[:, 0:T * HD].rearrange("p (t d) -> p t d", t=T))
                    if "output" in on and n in TURN_AT:
                        t = TURN_AT[n]
                        if t > 0:
                            wait_filled(act, i, f"op{t - 1}")
                        for k in range(2):
                            what = f"mix{t}.{k}"
                            empty(i, what, mixT[:, 4 * k:4 * k + 4, :],
                                  shared(what)[:].rearrange("p (c m) -> p c m", c=4))
                    if "project" in on and n == FIRST_EXPERT:
                        act.wait_ge(vec_gate, step(VEC_GATE, "rws", i - 1))
                        for k in range(2):
                            what = f"e0.{k}"
                            wait_read(act, i, f"e{NE - 1}.{k}")
                            wait_filled(act, i, what)
                            for t in (2 * k, 2 * k + 1):
                                ins = a.activation(acc[:, t, :], shared(what)[:, (t % 2) * QKV:(t % 2 + 1) * QKV],
                                                   ACT.Copy, scale=rws[:, t, 0:1])
                            ins.then_inc(freed(what), 1)
                    if "project" in on:
                        b = i - 1
                        if n == 2:
                            act.wait_ge(vec_proj, step(VEC_PROJ, "var", b))
                            a.activation(sm2[:, 1, :], sm2[:, 0, :], ACT.Ln).then_inc(act_proj, 1)
                            act.wait_ge(act_proj, step(ACT_PROJ, "ln", b))
                            a.activation(sm2[:, 2, :], sm2[:, 1, :], ACT.Exp, scale=-0.5).then_inc(act_proj, 1)
                        if n == 2:
                            act.wait_ge(vec_proj, step(VEC_PROJ, "nmr", b))
                            if "prepare" in stages_of(i - 1 if isinstance(i, int) else i):
                                act.wait_ge(vec_prep, step(VEC_PREP, "dt", i))
                            for t in range(T):
                                ins = a.activation(xh[:, t, :], x2a[:, t, :], ACT.Identity, scale=sm2[:, 4, t:t + 1],
                                                   bias=sm2[:, 5, t:t + 1])
                            ins.then_inc(act_proj, 1)
                            act.wait_ge(vec_proj, step(VEC_PROJ, "ssc", b))
                            a.activation(sm2[:, 8, :], sm2[:, 7, :], ACT.Ln, scale=2.0 ** 40).then_inc(act_proj, 1)
                            act.wait_ge(act_proj, step(ACT_PROJ, "ln2", b))
                            a.activation(sm2[:, 9, :], sm2[:, 8, :], ACT.Exp, scale=-0.5).then_inc(act_proj, 1)
                        if n == 5:
                            act.wait_ge(vec_gate, step(VEC_GATE, "shift", b))
                            a.activation(ex[:], g1[:, 8], ACT.Exp).then_inc(act_gate, 1)
                    if "prepare" in on:
                        b = i + 1
                        if n == 1:
                            act.wait_ge(vec_prep, step(VEC_PREP, "var", b))
                            a.activation(sm1[:, 1, :], sm1[:, 0, :], ACT.Ln).then_inc(act_prep, 1)
                            act.wait_ge(act_prep, step(ACT_PREP, "ln", b))
                            a.activation(sm1[:, 2, :], sm1[:, 1, :], ACT.Exp, scale=-0.5).then_inc(act_prep, 1)
                        if n == 5:
                            act.wait_ge(vec_prep, step(VEC_PREP, "nmr", b))
                            if "project" in on:
                                wait_filled(act, i, "xh.1")
                            for t in range(T):
                                ins = a.activation(xn[:, t, :], xt[:, t, :], ACT.Identity, scale=sm1[:, 4, t:t + 1],
                                                   bias=sm1[:, 5, t:t + 1])
                            ins.then_inc(act_prep, 1)
                        if n == 7:
                            wait(act, pool_prep, step(POOL_PREP, "u", i))
                            for k in range(CH):
                                empty(i, f"xn.{k}", xnT[:, k, :], shared(f"xn.{k}")[:])
                        if n == 9:
                            if isinstance(b, int) and b == 0:
                                act.wait_ge(pool_const, 4)
                            wait(act, b_kept, b * 16)
                            empty(i, "dtl", dtl[0:RANK + NS, :], shared("dtl")[0:RANK + NS, :])
                            wait(act, c_moved, b * 16)
                            empty(i, "c", c_next[:], shared("c")[:, 0:T * NS].rearrange("p (t k) -> p t k", t=T))
                        if n == 10:
                            act.wait_ge(pool_prep, step(POOL_PREP, "skip", b))
                            for k in range(CH):
                                wait_filled(act, i, f"dtp.{k}")
                                ins = a.activation(sp[:, k, :], shared(f"dtp.{k}")[:], ACT.Abs)
                            ins.then_inc(act_prep, 1)
                            wait(act, dt_moved, b * 16)
                            wait(act, pool_prep, step(POOL_PREP, "u", i))
                            for k in range(CH):
                                a.activation(dt_next[:, k, :], shared(f"dtp.{k}")[:],
                                             ACT.Relu).then_inc(freed(f"dtp.{k}"), 1)
                        if n == 11:
                            act.wait_ge(act_prep, step(ACT_PREP, "abs", b))
                            a.activation(sp[:], sp[:], ACT.Exp, scale=-1.0).then_inc(act_prep, 1)
                            act.wait_ge(act_prep, step(ACT_PREP, "exp", b))
                            a.activation(sp[:], sp[:], ACT.Ln, bias=1.0).then_inc(act_prep, 1)

            iterations(act, one)

        @block.vector
        def _(dve):
            w = nc.vector
            w.memset(wdt[:], 0.0).then_inc(vec_wdt, 1)
            dve.wait_ge(const_loaded, NCONST * 16)
            w.tensor_tensor(simsq[:], simf[:], simf[:], ALU.mult).then_inc(vec_setup, 1)

            def set_up(name):
                dve.wait_ge(vec_setup, step(VEC_SETUP, name, 0))

            dve.wait_ge(pe_const, 1)
            w.tensor_scalar(snorm[:, 0, :], mb[0][:, 0:NE], NORM_MIN_SQ, None, ALU.max).then_inc(vec_setup, 1)
            dve.wait_ge(act_setup, step(ACT_SETUP, "sqrt", 0))
            w.reciprocal(snorm[:, 2, :], snorm[:, 1, :]).then_inc(vec_setup, 1)
            set_up("inv")
            w.tensor_tensor(snorm[:, 2, :], snorm[:, 2, :], snorm[:, 0, :], ALU.mult).then_inc(vec_setup, 1)
            set_up("quot")
            w.tensor_tensor(snorm[:, 3, :], snorm[:, 2, :], snorm[:, 1, :], ALU.add).then_inc(vec_setup, 1)
            set_up("sum")
            w.tensor_scalar(snorm[:, 3, :], snorm[:, 3, :], 0.5 / SIM_SCALE, 1e-12 / SIM_SCALE, ALU.mult,
                            ALU.max).then_inc(vec_setup, 1)
            set_up("norm")
            w.reciprocal(snorm[:, 3, :], snorm[:, 3, :]).then_inc(vec_setup, 1)
            set_up("invnorm")
            w.tensor_tensor(simf[:], simf[:], snorm[:, 3, :].unsqueeze(1).broadcast_to([P, CH, NE]),
                            ALU.mult).then_inc(vec_setup, 1)
            dve.wait_ge(act_setup, step(ACT_SETUP, "expg", 0))
            w.tensor_scalar(negA[:], negA[:], -1.0, None, ALU.mult).then_inc(vec_setup, 1)
            w.tensor_scalar(sgate[:], sgate[:], 1.0, None, ALU.add).then_inc(vec_setup, 1)
            set_up("sg1")
            w.reciprocal(sgate[:], sgate[:]).then_inc(vec_setup, 1)
            dve.wait_ge(act_setup, step(ACT_SETUP, "simhi", 0))
            w.tensor_tensor(simlo[:], simf[:], simhi[:], ALU.subtract).then_inc(vec_setup, 1)
            set_up("simlo")
            dve.wait_ge(pool_const, 9)

            def split_weights(n):
                def at_step(name):
                    dve.wait_ge(vec_split, step(VEC_SPLIT, name, 0))

                if n in (1, 3):
                    c = (n - 1) // 2
                    if n == 1:
                        dve.wait_ge(weights_loaded, 16)
                    w.tensor_reduce(wmax[:, c:c + 1], wraw[:, c, :], AX_X, ALU.max,
                                    apply_absolute_value=True).then_inc(vec_split, 1)
                if n == 3:
                    at_step("max1")
                    w.tensor_tensor(wmax[:, 2:3], wmax[:, 0:1], wmax[:, 1:2], ALU.max).then_inc(vec_split, 1)
                if n == 5:
                    dve.wait_ge(pool_wmax, 1)
                    w.tensor_scalar(wmax[:, 4:5], wmax[:, 3:4], 1.0 / W_TOP, 1e-30, ALU.mult,
                                    ALU.max).then_inc(vec_split, 1)
                    at_step("unscale")
                    w.reciprocal(wmax[:, 5:6], wmax[:, 4:5]).then_inc(vec_split, 1)
                if n in (6, 8, 10, 12):
                    j = (n - 6) // 2
                    c, cols = weight_part(j)
                    dve.wait_ge(act_split, step(ACT_SPLIT, f"hi{j}", 0))
                    w.scalar_tensor_tensor(out=wlo[:, c, cols], in0=wraw[:, c, cols], scalar=wmax[:, 5:6],
                                           in1=whi[:, c, cols], op0=ALU.mult, op1=ALU.subtract).then_inc(vec_split, 1)

            def statistics(s, steps, b, src, st, mv, sm):
                for t in range(T):
                    ins = w.bn_stats(st[:, t, :], src[:, t, :])
                ins.then_inc(s, 1)
                dve.wait_ge(s, step(steps, "stats", b))
                stand(dve)
                for t in range(T):
                    ins = w.bn_aggr(mv[:, t, :], st[:, t, :])
                ins.then_inc(s, 1)
                dve.wait_ge(s, step(steps, "aggr", b))
                w.tensor_scalar(sm[:, 0, :], mv[:, :, 1], EPS, None, ALU.add).then_inc(s, 1)

            def newton_rstd(s, steps, b, mv, sm):
                w.tensor_tensor(sm[:, 3, :], sm[:, 2, :], sm[:, 2, :], ALU.mult).then_inc(s, 1)
                dve.wait_ge(s, step(steps, "sq", b))
                w.tensor_tensor(sm[:, 3, :], sm[:, 3, :], sm[:, 0, :], ALU.mult).then_inc(s, 1)
                dve.wait_ge(s, step(steps, "vsq", b))
                w.tensor_scalar(sm[:, 3, :], sm[:, 3, :], -0.5, 1.5, ALU.mult, ALU.add).then_inc(s, 1)
                dve.wait_ge(s, step(steps, "cor", b))
                w.tensor_tensor(sm[:, 4, :], sm[:, 2, :], sm[:, 3, :], ALU.mult).then_inc(s, 1)
                dve.wait_ge(s, step(steps, "rstd", b))
                w.scalar_tensor_tensor(out=sm[:, 5, :], in0=mv[:, :, 0], scalar=-1.0, in1=sm[:, 4, :], op0=ALU.mult,
                                       op1=ALU.mult).then_inc(s, 1)

            def scan(i, n, half):
                dve.wait_ge(abar_done, i * 2 * NS + 2 * n + half + 1)
                if half == 0:
                    dve.wait_ge(v_done, i * NS + n + 1)
                    wait(dve, hT_full, i * 2 * NS + 2 * (n - 1))
                w.tensor_tensor_scan(h[:, n % 2, half, :], abar[:, n % 2, half, :], v[:, n % 4, half, :], 0.0,
                                     ALU.mult, ALU.add).then_inc(scan_done, 1)

            def readout(i, n, k):
                dve.wait_ge(hT_full, i * 2 * NS + 2 * n + k + 1)
                if n == 0 and k == 0:
                    dve.wait_ge(pool_prep, step(POOL_PREP, "yinit", i))
                    wait(dve, read_out, i * READS)
                if n == 2 and k == 0:
                    dve.wait_ge(c_moved, (i + 1) * 16)
                if n == 0 and k == 1:
                    wait(dve, added_c, i * SCALES)
                if n > 0:
                    dve.wait_ge(read_out, read_by_vector(i, n - 1 - k, k))
                if n == NS - 1 and (not isinstance(i, int) or i > 0):
                    dve.wait_ge(act_proj, step(ACT_PROJ, "xh", i - 1))
                    dve.wait_ge(x2b_moved, i * 16)
                src = y_next if n == 0 else y
                dst = x2a if n == NS - 1 else y
                for t in (2 * k, 2 * k + 1):
                    ins = w.scalar_tensor_tensor(out=dst[:, t, :], in0=hT[n % 2][k][:, (t % 2) * D:(t % 2 + 1) * D],
                                                 scalar=(c_next if n < 2 else ccur)[:, t, n:n + 1], in1=src[:, t, :], op0=ALU.mult,
                                                 op1=ALU.add)
                ins.then_inc(read_out, 1)

            def combine(i, e):
                if e == 1:
                    dve.wait_ge(vec_gate, step(VEC_GATE, "rws", i - 1))
                if e == NE - 1 and "attend" in stages_of(i - 1):
                    wait_filled(dve, i - 1, "pv")
                for k in range(2):
                    what = f"e{e}.{k}"
                    wait_filled(dve, i, what)
                    wait_read(dve, late_from(i, e - 1) if e in LATE else i, f"e{e - 1}.{k}")
                    for t in (2 * k, 2 * k + 1):
                        src = shared(what)[:, (t % 2) * QKV:(t % 2 + 1) * QKV]
                        dst = qkv if e == NE - 1 else acc
                        ins = w.scalar_tensor_tensor(out=dst[:, t, :], in0=src, scalar=rws[:, t, e:e + 1],
                                                     in1=acc[:, t, :], op0=ALU.mult, op1=ALU.add)
                    ins.then_inc(freed(what), 1)

            def gating(i):
                b = i - 1
                k = vec_gate

                def at_step(name):
                    dve.wait_ge(k, step(VEC_GATE, name, b))

                dve.wait_ge(vec_proj, step(VEC_PROJ, "r", b))
                wait_filled(dve, i, "logit")
                for t in range(T):
                    ins = w.scalar_tensor_tensor(out=lg[:, t, :], in0=shared("logit")[:, t * NE:(t + 1) * NE],
                                                 scalar=sm2[:, 13, t:t + 1], in1=sgate[:], op0=ALU.mult,
                                                 op1=ALU.subtract)
                ins.then_inc(freed("logit"), 1)
                wait_read(dve, i, "logit")
                stand(dve)
                for t in range(T):
                    ins = w.max(top8[:, t, :], lg[:, t, :])
                ins.then_inc(k, 1)
                at_step("top")
                first, second = top8[:, :, 0], top8[:, :, 1]
                w.tensor_tensor(g1[:, 0], lg[:], over_experts(second), ALU.is_gt).then_inc(k, 1)
                w.tensor_tensor(g1[:, 1], lg[:], over_experts(second), ALU.is_equal).then_inc(k, 1)
                at_step("eq")
                w.tensor_tensor_scan(g1[:, 2].rearrange("p t e -> p (t e)"), restart[:].rearrange("p t e -> p (t e)"),
                                     g1[:, 1].rearrange("p t e -> p (t e)"), 0.0, ALU.mult, ALU.add).then_inc(k, 1)
                w.tensor_tensor(gs[:, 0, :], first, second, ALU.is_le).then_inc(k, 1)
                at_step("room")
                w.scalar_tensor_tensor(out=g1[:, 3], in0=g1[:, 2], scalar=-1.0, in1=over_experts(gs[:, 0, :]),
                                       op0=ALU.add, op1=ALU.is_le).then_inc(k, 1)
                at_step("fit")
                w.tensor_tensor(g1[:, 4], g1[:, 3], g1[:, 1], ALU.mult).then_inc(k, 1)
                at_step("take")
                w.tensor_tensor(g1[:, 4], g1[:, 4], g1[:, 0], ALU.add).then_inc(k, 1)
                w.tensor_scalar(gs[:, 1, :], first, 0.0, None, ALU.is_le).then_inc(k, 1)
                at_step("idle")
                w.tensor_tensor(g1[:, 5], g1[:, 4], over_experts(gs[:, 1, :]), ALU.mult).then_inc(k, 1)
                at_step("fbm")
                w.scalar_tensor_tensor(out=g1[:, 6], in0=lg[:], scalar=0.0, in1=g1[:, 5], op0=ALU.is_gt,
                                       op1=ALU.max).then_inc(k, 1)
                w.tensor_scalar(g1[:, 7], lg[:], 0.0, None, ALU.max).then_inc(k, 1)
                w.tensor_scalar(gs[:, 2, :], first, 0.0, None, ALU.max).then_inc(k, 1)
                at_step("gmax")
                w.tensor_tensor(g1[:, 8], g1[:, 7], over_experts(gs[:, 2, :]), ALU.subtract).then_inc(k, 1)

            def gating_end(i):
                b = i - 1
                k = vec_gate

                def at_step(name):
                    dve.wait_ge(k, step(VEC_GATE, name, b))

                dve.wait_ge(act_gate, b + 1)
                w.tensor_tensor(g1[:, 9], ex[:], g1[:, 6], ALU.mult).then_inc(k, 1)
                at_step("kept")
                w.tensor_reduce(gs[:, 3, :], g1[:, 9], AX_X, ALU.add).then_inc(k, 1)
                at_step("sum")
                w.reciprocal(gs[:, 4, :], gs[:, 3, :]).then_inc(k, 1)
                at_step("rsum")
                w.tensor_tensor(rw[:], g1[:, 9], over_experts(gs[:, 4, :]), ALU.mult).then_inc(k, 1)
                at_step("rw")
                w.tensor_scalar(rws[:], rw[:], wmax[:, 4:5], None, ALU.mult).then_inc(k, 1)

            def one(i):
                on, before = stages_of(i), stages_of(i - 1)
                for n in range(NS):
                    j, m = (i, n - 2) if n >= 2 else (i - 1, NS - 2 + n)
                    reads = "scan" in (on if n >= 2 else before)
                    if "project" in on and n == 2:
                        dve.wait_ge(read_out, i * READS)
                        dve.wait_ge(added_c, i * SCALES)
                        statistics(vec_proj, VEC_PROJ, i - 1, x2a, st2, mv2, sm2)
                    if "scan" in on:
                        scan(i, n, 0)
                    if reads:
                        readout(j, m, 0)
                    if "scan" in on:
                        scan(i, n, 1)
                    if reads and m % 2 == 0:
                        readout(j, m, 1)
                    experts = EXPERTS_AT.get(n, []) if "project" in on else []
                    for e in LATE_AT.get(n, []) if "attend" in on else []:
                        combine(i, e)
                    if isinstance(i, int) and i == 0:
                        split_weights(n)
                    if "attend" in on:
                        b = i - 2
                        if n == 0:
                            w.tensor_copy(rwb[:], rw[:]).then_inc(vec_att, 1)
                        if n in (6, 8):
                            for t in (n - 6, n - 5):
                                wait_filled(dve, i, f"s{t}")
                                w.tensor_reduce(mx[:, t:t + 1], shared(f"s{t}")[:, 0:(t + 1) * P], AX_X,
                                                ALU.max).then_inc(vec_att, 1)
                                dve.wait_ge(vec_att, step(VEC_ATT, f"mx{t}", b))
                                w.tensor_scalar(nb[:, t:t + 1], mx[:, t:t + 1], -(HD ** -0.5), None,
                                                ALU.mult).then_inc(vec_att, 1)
                        if n == 9:
                            wait_read(dve, i, "s2")
                            wait_read(dve, i, "s3")
                            w.reciprocal(rinv[:], rs[:]).then_inc(vec_att, 1)
                            dve.wait_ge(vec_att, step(VEC_ATT, "rinv", b))
                            wait(dve, mixed, b * T)
                            w.tensor_tensor(rwn[:], rwb[:], over_experts(rinv[:]), ALU.mult).then_inc(vec_att, 1)
                    if "output" in on and n in RESIDUAL_AT:
                        t = RESIDUAL_AT[n]
                        if t == 0:
                            wait(dve, out_stored, (i - 3) * 16)
                            dve.wait_ge(x2c_moved, (i - 2) * 16)
                        wait_filled(dve, i, f"op{t}")
                        w.tensor_tensor(outt[:, t, :], shared(f"op{t}")[:, 0:D], x2c[:, t, :],
                                        ALU.add).then_inc(freed(f"op{t}"), 1)
                    if "project" in on and n == 6:
                        gating_end(i)
                    for e in experts[:1]:
                        if e > 0:
                            combine(i, e)
                    if "project" in on:
                        b = i - 1
                        if n == 2:
                            dve.wait_ge(act_proj, step(ACT_PROJ, "y0", b))
                            newton_rstd(vec_proj, VEC_PROJ, b, mv2, sm2)
                            w.tensor_tensor(sm2[:, 6, :], sm2[:, 4, :], sm2[:, 4, :], ALU.mult).then_inc(vec_proj, 1)
                            dve.wait_ge(vec_proj, step(VEC_PROJ, "rr", b))
                            w.scalar_tensor_tensor(out=sm2[:, 6, :], in0=sm2[:, 6, :], scalar=float(D),
                                                   in1=mv2[:, :, 1], op0=ALU.mult, op1=ALU.mult).then_inc(vec_proj, 1)
                            dve.wait_ge(vec_proj, step(VEC_PROJ, "ss", b))
                            w.tensor_scalar(sm2[:, 7, :], sm2[:, 6, :], NORM_MIN_SQ, None,
                                            ALU.max).then_inc(vec_proj, 1)
                        if n == 3:
                            dve.wait_ge(act_proj, step(ACT_PROJ, "y2", b))
                            w.tensor_scalar(sm2[:, 10, :], sm2[:, 9, :], 2.0 ** 20, None,
                                            ALU.mult).then_inc(vec_proj, 1)
                            dve.wait_ge(vec_proj, step(VEC_PROJ, "y", b))
                            w.tensor_tensor(sm2[:, 11, :], sm2[:, 10, :], sm2[:, 10, :], ALU.mult).then_inc(vec_proj, 1)
                            dve.wait_ge(vec_proj, step(VEC_PROJ, "ysq", b))
                            w.tensor_tensor(sm2[:, 11, :], sm2[:, 11, :], sm2[:, 7, :], ALU.mult).then_inc(vec_proj, 1)
                            dve.wait_ge(vec_proj, step(VEC_PROJ, "yv", b))
                            w.tensor_scalar(sm2[:, 12, :], sm2[:, 11, :], -0.5, 1.5, ALU.mult,
                                            ALU.add).then_inc(vec_proj, 1)
                            dve.wait_ge(vec_proj, step(VEC_PROJ, "ycor", b))
                            w.scalar_tensor_tensor(out=sm2[:, 13, :], in0=sm2[:, 10, :], scalar=1.0 / SIM_SCALE,
                                                   in1=sm2[:, 12, :], op0=ALU.mult, op1=ALU.mult).then_inc(vec_proj, 1)
                        if n == 3:
                            for k in range(CH):
                                dve.wait_ge(act_proj, step(ACT_PROJ, f"hi{k}", b))
                                w.tensor_tensor(xlo[:, k, :], shared(f"xh.{k}")[:], xhi[:, k, :],
                                                ALU.subtract).then_inc(freed(f"xh.{k}"), 1)
                        if n == 5:
                            gating(i)
                    if "prepare" in on:
                        b = i + 1
                        if n == 0:
                            dve.wait_ge(x_loaded, (b + 1) * 16)
                            statistics(vec_prep, VEC_PREP, b, xt, st1, mv1, sm1)
                        if n == 4:
                            dve.wait_ge(act_prep, step(ACT_PREP, "y0", b))
                            newton_rstd(vec_prep, VEC_PREP, b, mv1, sm1)
                        if n == 12:
                            dve.wait_ge(act_prep, step(ACT_PREP, "softplus", b))
                            w.tensor_tensor(dt_next[:], dt_next[:], sp[:], ALU.add).then_inc(vec_prep, 1)
                    for e in experts[1:]:
                        combine(i, e)

            iterations(dve, one)

        @block.tensor
        def _(pe):
            m = nc.tensor
            pe.wait_ge(const_loaded, NCONST * 16)
            pe.wait_ge(pool_const, 9)
            pe.wait_ge(vec_setup, step(VEC_SETUP, "simsq", 0))
            for k in range(CH):
                ins = m.matmul(mb[0][:, 0:NE], ones[:], simsq[:, k, :], start=k == 0, stop=k == CH - 1)
            ins.then_inc(pe_const, 1)
            pe.wait_ge(vec_setup, len(VEC_SETUP))

            def claim(i, what):
                wait(pe, freed(what), bank_use(i, what) - 1)

            def turn_h(i, n):
                pe.wait_ge(scan_done, i * 2 * NS + 2 * n + 2)
                for k in range(2):
                    if k == 1 and n % 2 == 1:
                        wait(pe, scaled_c, i * SCALES + n // 2)
                    else:
                        wait(pe, read_out, read_by_vector(i, n - 2, k))
                    for t in (2 * k, 2 * k + 1):
                        for half in range(CH):
                            c = (t % 2) * D + half * P
                            ins = m.transpose(hT[n % 2][k][:, c:c + P], h[:, n % 2, half, t * P:(t + 1) * P], ident[:])
                    ins.then_inc(hT_full, 1)

            def project(i, e):
                for k in range(2):
                    what = f"e{e}.{k}"
                    claim(i, what)
                    for t in (2 * k, 2 * k + 1):
                        dst = shared(what)[:, (t % 2) * QKV:(t % 2 + 1) * QKV]
                        parts = [(s, wt, c) for c in range(CH) for s, wt in ((xhi, whi), (xhi, wlo), (xlo, whi))]
                        for j, (s, wt, c) in enumerate(parts):
                            ins = m.matmul(dst, s[:, c, t * P:(t + 1) * P], wt[:, c, e * QKV:(e + 1) * QKV],
                                           start=j == 0, stop=j == len(parts) - 1)
                    ins.then_inc(filled(what), 1)

            def scores(i, t):
                what = f"s{t}"
                claim(i, what)
                w = (t + 1) * P
                m.matmul(shared(what)[:, 0:w], qT[:, t * P:(t + 1) * P], kT[:, 0:w], start=True, stop=False)
                m.matmul(shared(what)[:, t * P:w], identb[:], causal[:], start=False, stop=True).then_inc(filled(what), 1)

            def turn_mix(i, t):
                pe.wait_ge(mixed, (i - 3) * T + t + 1)
                for k in range(2):
                    what = f"mix{t}.{k}"
                    claim(i, what)
                    for c in range(4):
                        e = 2 * (4 * k + c)
                        ins = m.transpose(shared(what)[:, c * P:(c + 1) * P],
                                          mix[:, t % 2, e:e + 2, :].rearrange("p e d -> p (e d)"), ident[:])
                    ins.then_inc(filled(what), 1)

            def out_projection(i, t):
                what = f"op{t}"
                claim(i, what)
                wait_read(pe, i, f"mix{t}.0")
                wait_read(pe, i, f"mix{t}.1")
                for j in range(KO):
                    ins = m.matmul(shared(what)[:, 0:D], mixT[:, j, :], wo[:, j, :], start=j == 0, stop=j == KO - 1)
                ins.then_inc(filled(what), 1)

            def turn(i, what, src):
                claim(i, what)
                stand(pe)
                for c, block_ in enumerate(src):
                    ins = m.transpose(shared(what)[0:block_.shape[1], c * P:(c + 1) * P], block_, ident[:])
                ins.then_inc(filled(what), 1)

            def one(i):
                on, before = stages_of(i), stages_of(i - 1)
                for n in range(NS):
                    if n == 0 and "scan" in before:
                        turn_h(i - 1, NS - 1)
                    if n > 0 and "scan" in on:
                        turn_h(i, n - 1)
                    for e in LATE_AT.get(n, []) if "attend" in on else []:
                        project(i, e)
                    experts = EXPERTS_AT.get(n, []) if "project" in on else []
                    if "project" in on:
                        if n == 3:
                            pe.wait_ge(act_proj, step(ACT_PROJ, "xh", i - 1))
                            for k in range(CH):
                                turn(i, f"xh.{k}", [xh[:, t, k * P:(k + 1) * P] for t in range(T)])
                        if n == 5:
                            claim(i, "logit")
                            wait_read(pe, i, "xh.0")
                            wait_read(pe, i, "xh.1")
                            for t in range(T):
                                parts = [(s, wt, c) for c in range(CH)
                                         for s, wt in ((xhi, simhi), (xhi, simlo), (xlo, simhi))]
                                for j, (s, wt, c) in enumerate(parts):
                                    ins = m.matmul(shared("logit")[:, t * NE:(t + 1) * NE], s[:, c, t * P:(t + 1) * P],
                                                   wt[:, c, :], start=j == 0, stop=j == len(parts) - 1)
                            ins.then_inc(filled("logit"), 1)
                    if "attend" in on:
                        if n == 5:
                            for k in range(2):
                                wait_read(pe, i, f"e{NE - 1}.{k}")
                            for k in range(2):
                                turn(i, "qk"[k], [qkv[:, t, k * HD:(k + 1) * HD] for t in range(T)])
                        if n in (6, 8):
                            if n == 6:
                                wait_read(pe, i, "q")
                                wait_read(pe, i, "k")
                            scores(i, n - 6)
                            scores(i, n - 5)
                        if n == 11:
                            wait_read(pe, i, "s2")
                            wait_read(pe, i, "s3")
                            turn(i, "pt1", [pr[:, t, P:2 * P] for t in range(1, T)])
                            turn(i, "pt0", [pr[:, t, 0:P] for t in range(T)])
                        if n == 12:
                            turn(i, "pt23", [pr[:, 2, 2 * P:3 * P], pr[:, 3, 2 * P:3 * P], pr[:, 3, 2 * P:3 * P],
                                             pr[:, 3, 3 * P:4 * P]])
                        if n == 13:
                            claim(i, "pv")
                            for what in ("pt1", "pt0", "pt23"):
                                wait_read(pe, i, what)
                            for t in range(T):
                                for j in range(t + 1):
                                    ins = m.matmul(shared("pv")[:, t * HD:(t + 1) * HD], pt[:, j, t * P:(t + 1) * P],
                                                   qkv[:, j, 2 * HD:3 * HD], start=j == 0, stop=j == t)
                            ins.then_inc(filled("pv"), 1)
                    if "output" in on:
                        if isinstance(i, int) and i == 3 and n == min(OUT_AT):
                            pe.wait_ge(wo_loaded, 16)
                        if n in OUT_AT:
                            out_projection(i, OUT_AT[n])
                        if n in TURN_AT:
                            turn_mix(i, TURN_AT[n])
                    if isinstance(i, int) and i == 1 and n == FIRST_EXPERT:
                        pe.wait_ge(vec_split, len(VEC_SPLIT))
                    for e in experts[:1]:
                        project(i, e)
                    if "prepare" in on:
                        if n == 7:
                            pe.wait_ge(act_prep, step(ACT_PREP, "xn", i + 1))
                            for k in range(CH):
                                turn(i, f"xn.{k}", [xn[:, t, k * P:(k + 1) * P] for t in range(T)])
                        if n == 9:
                            claim(i, "dtl")
                            wait_read(pe, i, "xn.0")
                            wait_read(pe, i, "xn.1")
                            for k in range(CH):
                                ins = m.matmul(shared("dtl")[0:RANK + NS, :], wx[:, k, 0:RANK + NS], xnT[:, k, :],
                                               start=k == 0, stop=k == CH - 1)
                            ins.then_inc(filled("dtl"), 1)
                            claim(i, "c")
                            for t in range(T):
                                for k in range(CH):
                                    ins = m.matmul(shared("c")[:, t * NS:(t + 1) * NS], xnT[:, k, t * P:(t + 1) * P],
                                                   wx[:, k, RANK + NS:], start=k == 0, stop=k == CH - 1)
                            ins.then_inc(filled("c"), 1)
                        if n == 10:
                            wait_read(pe, i, "dtl")
                            for k in range(CH):
                                claim(i, f"dtp.{k}")
                                m.matmul(shared(f"dtp.{k}")[:], wdt[:, k * P:(k + 1) * P], dtl[:], start=True,
                                         stop=True).then_inc(filled(f"dtp.{k}"), 1)
                    for e in experts[1:]:
                        project(i, e)

            iterations(pe, one)


_OUT = (NB, L, D)


def kernel(**inputs):
    import numpy as np
    import concourse.bacc as bacc
    from concourse.bass_utils import run_bass_kernel_spmd

    def take(name):
        return np.asarray(inputs[name])

    arrays = {
        "x": take("L0_attn_x"),
        "A_log": take("L0_attn_A_log"),
        "D_param": take("L0_attn_D_param").reshape(1, D),
        "WxT": take("L0_attn_W_x").T,
        "WdtT": take("L0_attn_W_dt").T,
        "b_dt": take("L0_attn_b_dt").reshape(1, D),
        "sim": take("L0_ffn_sim_matrix"),
        "gates": take("L0_ffn_gates").reshape(1, NE),
        "Wqkv": np.stack([take(f"L0_ffn_{n}_proj") for n in "qkv"], 2).transpose(1, 0, 2, 3).reshape(D, NE * QKV),
        "Wo": take("L0_ffn_o_proj").reshape(NE * HD, D),
    }
    arrays = {k: np.ascontiguousarray(a) for k, a in arrays.items()}
    nc = bacc.Bacc("TRN2", target_bir_lowering=False, num_devices=1)
    args = [nc.dram_tensor(f"{k}_dram", a.shape, mybir.dt.from_np(a.dtype), kind="ExternalInput").ap()
            for k, a in arrays.items()]
    args.append(nc.dram_tensor("b_rows", (NS, L), F32, kind="Internal").ap())
    args.append(nc.dram_tensor("out_dram", _OUT, F32, kind="ExternalOutput").ap())
    scan_attention_kernel(nc, *args)
    r = run_bass_kernel_spmd(nc, [{f"{k}_dram": a for k, a in arrays.items()}], core_ids=[0])
    return r.results[0]["out_dram"]
```
